# Optimizing a Trainium2 kernel written in Bass

```python
import numpy as np
import jax
import jax.numpy as jnp

def _softmax(x, axis=-1):
    return jax.nn.softmax(x, axis=axis)

def _gelu(x):
    return jax.nn.gelu(x, approximate=True)

def _silu(x):
    return jax.nn.silu(x)

def _sigmoid(x):
    return jax.nn.sigmoid(x)

def _layernorm(x, axis=-1, eps=1e-05):
    m = jnp.mean(x, axis=axis, keepdims=True)
    v = jnp.var(x, axis=axis, keepdims=True)
    return (x - m) / jnp.sqrt(v + eps)

def _scatter_add(tgt, idx, src, axis=0):
    return tgt.at[idx].add(src)

def _segment_sum(src, seg, n):
    return jax.ops.segment_sum(src, seg, n)
kernel_name = 'mk_flamingo_gated_d1_seqx_r2_3557a7'

def setup_inputs(seed: int=0):
    np.random.seed(seed)
    _w = jnp.asarray

    def _rec_inputs():
        import jax
        import jax.numpy as jnp
        _rk = jax.random.key(seed)
        x = -0.0002928 + 1 * jax.random.normal(jax.random.fold_in(_rk, 1), (16, 512, 512), jnp.float32)
        _lenS = 512 - jax.random.randint(jax.random.fold_in(_rk, 7), (16,), 0, max(1, 512 // 4) + 1, jnp.int32)
        _lenS2 = 512 - jax.random.randint(jax.random.fold_in(_rk, 8), (16,), 0, max(1, 512 // 4) + 1, jnp.int32)
        _ctx_1024P = jax.random.normal(jax.random.fold_in(_rk, 11), (16, 16, 512), jnp.float32)
        _ctx_1024c = jax.random.dirichlet(jax.random.fold_in(_rk, 511), 0.3 * jnp.ones((16,), jnp.float32), (16, 512))
        _ctx_1024t = jnp.einsum('bsk,bkd->bsd', _ctx_1024c, _ctx_1024P)
        _ctx_1024t = _ctx_1024t * jax.lax.rsqrt(jnp.mean(jnp.square(_ctx_1024t)) + 1e-12) * 0.953939
        ctx_1024 = -1.39393e-06 + 0.999914 * (_ctx_1024t + 0.3 * jax.random.normal(jax.random.fold_in(_rk, 611), (16, 512, 512), jnp.float32))
        _g = jax.random.normal(jax.random.fold_in(_rk, 9001), (2, 1), jnp.float32)
        _g = jnp.sign(_g) * jnp.maximum(jnp.abs(_g), 1.0) + (_g == 0) * 1.0
        g_xattn = _g[0]
        g_ffn = _g[1]
        return (x, ctx_1024, g_xattn, g_ffn)
    x, ctx_1024, g_xattn, g_ffn = _rec_inputs()

    def _L0_xattn_setup():
        import jax, jax.numpy as jnp
        import numpy as np
        B, S, D = (1, 2048, 512)
        NUM_HEADS, HEAD_DIM = (16, 64)
        WINDOW = 128
        EMBED = NUM_HEADS * HEAD_DIM
        key = jax.random.key(seed)
        ks = jax.random.split(key, 7)
        scale_in = 1.0 / np.sqrt(D)
        scale_e = 1.0 / np.sqrt(EMBED)
        return {'query': jax.random.normal(ks[0], (B, S, D), dtype=jnp.float32), 'key': jax.random.normal(ks[1], (B, S, D), dtype=jnp.float32), 'value': jax.random.normal(ks[2], (B, S, D), dtype=jnp.float32), 'Wq': jax.random.normal(ks[3], (D, EMBED), dtype=jnp.float32) * scale_in, 'Wk': jax.random.normal(ks[4], (D, EMBED), dtype=jnp.float32) * scale_in, 'Wv': jax.random.normal(ks[5], (D, EMBED), dtype=jnp.float32) * scale_in, 'Wo': jax.random.normal(ks[6], (EMBED, D), dtype=jnp.float32) * scale_e}
    _L0_xattn_all = _L0_xattn_setup()
    _L0_xattn_in = {k: v for k, v in _L0_xattn_all.items() if k in ('Wq', 'Wk', 'Wv', 'Wo')}
    del _L0_xattn_all

    def _L0_ffn_setup():
        import jax, jax.numpy as jnp
        import numpy as np
        DIM = 512

        def _reference_tuple_inner(x, W_r, W_k, W_v, mu_r, mu_k):
            B, T, C = x.shape
            x_prev = jnp.concatenate([jnp.zeros((B, 1, C), x.dtype), x[:, :-1, :]], axis=1)
            xr = mu_r * x + (1.0 - mu_r) * x_prev
            xk = mu_k * x + (1.0 - mu_k) * x_prev
            r = jax.nn.sigmoid(jnp.einsum('btc,dc->btd', xr, W_r))
            k = jnp.einsum('btc,dc->btd', xk, W_k)
            k_act = jnp.square(jax.nn.relu(k))
            out = r * jnp.einsum('btc,dc->btd', k_act, W_v)
            new_state = x[:, -1, :]
            return (out, new_state)
        key = jax.random.key(seed)
        ks = jax.random.split(key, 6)
        B, T, C = (8, 1024, DIM)
        x = jax.random.normal(ks[0], (B, T, C), dtype=jnp.float32)
        s = 1.0 / np.sqrt(C)
        W_r = jax.random.uniform(ks[1], (C, C), jnp.float32, -s, s)
        W_k = jax.random.uniform(ks[2], (C, C), jnp.float32, -s, s)
        W_v = jax.random.uniform(ks[3], (C, C), jnp.float32, -s, s)
        mu_r = jax.random.uniform(ks[4], (C,), jnp.float32)
        mu_k = jax.random.uniform(ks[5], (C,), jnp.float32)
        return {'x': x, 'W_r': W_r, 'W_k': W_k, 'W_v': W_v, 'mu_r': mu_r, 'mu_k': mu_k}
    _L0_ffn_all = _L0_ffn_setup()
    _L0_ffn_in = {k: v for k, v in _L0_ffn_all.items() if k in ('W_r', 'W_k', 'W_v', 'mu_r', 'mu_k')}
    del _L0_ffn_all
    return {'x': x, 'ctx_1024': ctx_1024, 'g_xattn': g_xattn, 'g_ffn': g_ffn, 'L0_xattn_Wq': _L0_xattn_in['Wq'], 'L0_xattn_Wk': _L0_xattn_in['Wk'], 'L0_xattn_Wv': _L0_xattn_in['Wv'], 'L0_xattn_Wo': _L0_xattn_in['Wo'], 'L0_ffn_W_r': _L0_ffn_in['W_r'], 'L0_ffn_W_k': _L0_ffn_in['W_k'], 'L0_ffn_W_v': _L0_ffn_in['W_v'], 'L0_ffn_mu_r': _L0_ffn_in['mu_r'], 'L0_ffn_mu_k': _L0_ffn_in['mu_k']}

def reference(x, ctx_1024, g_xattn, g_ffn, L0_xattn_Wq, L0_xattn_Wk, L0_xattn_Wv, L0_xattn_Wo, L0_ffn_W_r, L0_ffn_W_k, L0_ffn_W_v, L0_ffn_mu_r, L0_ffn_mu_k):
    import jax
    import jax.numpy as jnp

    def _L0_xattn_ref(query, key, value, Wq, Wk, Wv, Wo):
        import jax, jax.numpy as jnp
        import numpy as np
        B, S, D = (1, 2048, 512)
        NUM_HEADS, HEAD_DIM = (16, 64)
        WINDOW = 128
        EMBED = NUM_HEADS * HEAD_DIM
        Bq, Sq, _ = query.shape
        q = (query @ Wq).reshape(Bq, Sq, NUM_HEADS, HEAD_DIM).transpose(0, 2, 1, 3)
        k = (key @ Wk).reshape(Bq, Sq, NUM_HEADS, HEAD_DIM).transpose(0, 2, 1, 3)
        v = (value @ Wv).reshape(Bq, Sq, NUM_HEADS, HEAD_DIM).transpose(0, 2, 1, 3)
        idx = jnp.arange(Sq)
        local_mask = jnp.abs(idx[:, None] - idx[None, :]) > WINDOW
        scores = jnp.einsum('bhqd,bhkd->bhqk', q, k) / jnp.sqrt(jnp.float32(HEAD_DIM))
        scores = jnp.where(local_mask, -jnp.inf, scores)
        attn = jax.nn.softmax(scores, axis=-1)
        out = jnp.einsum('bhqk,bhkd->bhqd', attn, v)
        out = out.transpose(0, 2, 1, 3).reshape(Bq, Sq, EMBED)
        return out @ Wo

    def _L0_ffn_ref(x, W_r, W_k, W_v, mu_r, mu_k):
        import jax, jax.numpy as jnp
        import numpy as np
        DIM = 512

        def _reference_tuple_inner(x, W_r, W_k, W_v, mu_r, mu_k):
            B, T, C = x.shape
            x_prev = jnp.concatenate([jnp.zeros((B, 1, C), x.dtype), x[:, :-1, :]], axis=1)
            xr = mu_r * x + (1.0 - mu_r) * x_prev
            xk = mu_k * x + (1.0 - mu_k) * x_prev
            r = jax.nn.sigmoid(jnp.einsum('btc,dc->btd', xr, W_r))
            k = jnp.einsum('btc,dc->btd', xk, W_k)
            k_act = jnp.square(jax.nn.relu(k))
            out = r * jnp.einsum('btc,dc->btd', k_act, W_v)
            new_state = x[:, -1, :]
            return (out, new_state)
        return _reference_tuple_inner(x, W_r, W_k, W_v, mu_r, mu_k)[0]
    x = x + jnp.tanh(g_xattn[0]) * _L0_xattn_ref(_layernorm(x, axis=-1), ctx_1024, ctx_1024, L0_xattn_Wq, L0_xattn_Wk, L0_xattn_Wv, L0_xattn_Wo)
    x = x + jnp.tanh(g_ffn[0]) * _L0_ffn_ref(_layernorm(x, axis=-1), L0_ffn_W_r, L0_ffn_W_k, L0_ffn_W_v, L0_ffn_mu_r, L0_ffn_mu_k)
    return x

_drawn_inputs = setup_inputs


def setup_inputs(seed=0):
    import zlib

    import numpy as np

    out = dict(_drawn_inputs(seed))
    spreads = {}
    factors = {'L0_ffn_W_r': 3.3, 'L0_ffn_mu_r': 7.44}
    for name, (base, spread) in spreads.items():
        noise = np.random.default_rng([zlib.crc32(name.encode()), seed]).standard_normal(out[name].shape)
        drawn = base * np.exp(spread * noise) if base else spread * noise
        out[name] = jnp.asarray(drawn.astype(out[name].dtype))
    for name, factor in factors.items():
        out[name] = (out[name] * factor).astype(out[name].dtype)
    return out
```

```python
from contextlib import ExitStack

import concourse.bass as bass
from concourse import mybir

F32 = mybir.dt.float32
F32R = mybir.dt.float32r
ALU = mybir.AluOpType
ACT = mybir.ActivationFunctionType

P = 128
HEAD = 64
WINDOW = 128
EPS = 1e-5
MASKED = -1e30
LARGEST = 3e38
HI, LO = 0, 1
PRODUCTS = ((HI, HI), (HI, LO), (LO, HI))

TILES = 4
KEYS_OF = [range(max(i - 1, 0), min(i + 2, TILES)) for i in range(TILES)]
FIRST = [sum(len(KEYS_OF[a]) for a in range(i)) for i in range(TILES)]
BLOCKS = sum(len(k) for k in KEYS_OF)
GROUPS = [(0, 4, 1), (4, 4, 2), (8, 2, 3)]


def wait_alone(eng, sem, value, passed):
    eng.wait_ge(sem, value)
    eng.sem_inc(passed, 1)


def block_of(q, k):
    return FIRST[q] + k - KEYS_OF[q][0]


PAIRS = 8
INPUT_JOBS = [("ctx", 0), ("ctx", 1), ("x", 0), ("x", 1), ("ctx", 2), ("ctx", 3), ("x", 2), ("x", 3)]


def qk_jobs(pair):
    return [("q", pair), ("k", pair)]


def v_jobs(group):
    return [("v", group, t) for t in range(TILES)]


HEAD_JOBS = INPUT_JOBS + qk_jobs(0) + v_jobs(0) + qk_jobs(1)
OWN_JOBS = qk_jobs(2) + qk_jobs(3) + qk_jobs(4) + qk_jobs(5) + v_jobs(1) + qk_jobs(6) + qk_jobs(7)
LOOP_JOBS = OWN_JOBS + [("next",) + j for j in HEAD_JOBS[:10] + qk_jobs(1) + v_jobs(0)]


def attention(nc, x, ctx_in, wq, wk, wv, heads_out):
    batches = x.shape[0]
    D = x.shape[3]
    E = wq.shape[2]
    DT = D // P
    VH = D // HEAD
    assert E == PAIRS * P and DT == TILES and VH == 8

    with ExitStack() as es:
        def sb(name, shape, dt=F32):
            return es.enter_context(nc.sbuf_tensor(name, shape, dt))

        def ps(name, shape):
            return es.enter_context(nc.psum_tensor(name, shape, F32))

        def sem(name):
            return es.enter_context(nc.semaphore(name))

        w = {n: sb(f"w{n}_parts", [P, 2, DT, E], F32R) for n in "qkv"}
        inT = {n: sb(f"{n}T", [P, 2, DT, TILES * P], F32R) for n in ("ctx", "x")}
        qT = sb("qT", [P, 2, 2, TILES * P], F32R)
        kT = sb("kT", [P, 2, 2, TILES * P], F32R)
        v = sb("v", [P, TILES, VH, 2, HEAD], F32R)
        raw = {n: sb(f"raw_{n}", [P, 2, D]) for n in ("ctx", "x")}
        probs = sb("probs", [P, 2, BLOCKS * P])
        pT = sb("pT", [P, 2, 2, BLOCKS, P], F32R)
        low_half = sb("low_half", [HEAD, TILES * P])
        out_sb = sb("out_sb", [P, 2, TILES * P])
        band = sb("band", [P, 3 * P])
        ident = sb("ident", [P, P])
        neg_max = sb("neg_max", [P, 8])
        sums = sb("sums", [P, 8])
        inv_sums = sb("inv_sums", [P, 8])
        stats = sb("stats", [P, TILES, 6])
        mean_var = sb("mean_var", [P, TILES, 2])
        var_eps = sb("var_eps", [P, TILES])
        rstd = sb("rstd", [P, TILES])
        minus_half = sb("minus_half", [P, 2])

        job_ps = [ps(f"job{i}", [P, 512]) for i in range(2)]
        score_ps = [ps(f"score{i}", [P, 512]) for i in range(2)]
        tr_ps = [ps(f"tr{i}", [P, 512]) for i in range(2)]
        out_ps = [ps(f"out{i}", [P, 512]) for i in range(2)]

        dve_passed = sem("dve_passed")
        pool_passed = sem("pool_passed")
        filled = sem("filled")
        const_done = sem("const_done")
        w_loaded = [sem(f"w_loaded{i}") for i in range(4)]
        w_hi = sem("w_hi")
        w_lo = sem("w_lo")
        in_loaded = {n: [sem(f"{n}_loaded{i}") for i in range(2)] for n in ("ctx", "x")}
        ln_step = sem("ln_step")
        rstd_ready = sem("rstd_ready")
        x_normed = sem("x_normed")
        job_full = sem("job_full")
        job_hi = sem("job_hi")
        job_done = sem("job_done")
        scored = sem("scored")
        masked = sem("masked")
        exped = sem("exped")
        inverted = sem("inverted")
        normed = sem("normed")
        tr_full = sem("tr_full")
        tr_hi = sem("tr_hi")
        tr_done = sem("tr_done")
        pv_full = sem("pv_full")
        pv_half = sem("pv_half")
        pv_done = sem("pv_done")
        stored = [sem(f"stored{i}") for i in range(2)]

        def job_value(b, job):
            if b is None:
                return HEAD_JOBS.index(job) + 1
            return len(LOOP_JOBS) * b + (len(HEAD_JOBS) + LOOP_JOBS.index(job) + 1)

        def job_bank(b, job):
            n = HEAD_JOBS.index(job) if b is None else len(HEAD_JOBS) + LOOP_JOBS.index(job)
            return job_ps[n % 2]

        def pair_value(b, pair, per, n):
            return per * PAIRS * b + (per * pair + n) if b is not None else per * pair + n

        def score_span(i):
            return slice(FIRST[i] * P, (FIRST[i] + len(KEYS_OF[i])) * P)

        chunks = [(n, d, half) for n in "qkv" for d in range(DT) for half in range(E // 512)]
        stage = probs[:, :, :].rearrange("p h n -> p (h n)")[:, 0:4 * 512].rearrange("p (s n) -> p s n", s=4)

        block = es.enter_context(nc.Block())

        @block.sync
        def _(sp):
            def load(b, name, t):
                src = (ctx_in if name == "ctx" else x)[b, t]
                sp.dma_start(raw[name][:, t % 2, :], src).then_inc(in_loaded[name][t % 2], 16)

            def load_second(b_jobs, b, prefix):
                for name, t in (("ctx", 2), ("ctx", 3), ("x", 2), ("x", 3)):
                    sp.wait_ge(job_full, job_value(b_jobs, prefix + (name, t - 2)))
                    load(b, name, t)

            for name, t in INPUT_JOBS[:4]:
                load(0, name, t)
            for c, (n, d, half) in enumerate(chunks):
                if c >= 4:
                    sp.wait_ge(w_lo, c - 3)
                src = {"q": wq, "k": wk, "v": wv}[n][d, :, half * 512:(half + 1) * 512]
                sp.dma_start(stage[:, c % 4, :], src).then_inc(w_loaded[c % 4], 16)
                if c == 7:
                    load_second(None, 0, ())
            for s in stored:
                sp.sem_inc(s, 16)

            def store(b, pair):
                sp.wait_ge(pv_done, pair_value(b, pair, 2, 2) + 2)
                sp.dma_start(heads_out[b, :, :, pair, :].rearrange("t p n -> p t n"),
                             out_sb[:, pair % 2, :].rearrange("p (t n) -> p t n", n=P)).then_inc(stored[pair % 2], 16)

            def batch(b, last):
                if not last:
                    for name, t in INPUT_JOBS[:4]:
                        sp.wait_ge(job_full, len(LOOP_JOBS) * b + 8)
                        load(b + 1, name, t)
                for pair in range(PAIRS):
                    if pair == 6 and not last:
                        load_second(b, b + 1, ("next",))
                    store(b, pair)

            with sp.Fori(0, batches - 1) as b:
                batch(b, False)
            batch(batches - 1, True)
            for s in stored:
                sp.wait_ge(s, 16 * (1 + batches * PAIRS // 2))

        @block.tensor
        def _(pe):
            def input_job(b, job, src_b):
                name, t = job[-2:]
                value = job_value(b, job)
                bank = job_bank(b, job)
                if b is not None or HEAD_JOBS.index(job) >= 2:
                    pe.wait_ge(job_done, value - 2)
                if name == "ctx":
                    pe.wait_ge(in_loaded["ctx"][t % 2], 32 * src_b + 16 * (t // 2 + 1))
                else:
                    pe.wait_ge(x_normed, TILES * src_b + t + 1)
                for d in range(DT):
                    last = pe.transpose(bank[:, d * P:(d + 1) * P], raw[name][:, t % 2, d * P:(d + 1) * P], ident[:, :])
                last.then_inc(job_full, 1)

            def project(b, job, half=None):
                name, pair = job[-2:]
                bank = job_bank(b, job)
                if half != 1:
                    pe.wait_ge(job_done, job_value(b, job) - 2)
                src = inT["x" if name == "q" else "ctx"]
                steps = [(d, a, c) for d in range(DT) for a, c in PRODUCTS]
                n = len(steps) // 2
                for s in {None: range(2 * n), 0: range(n), 1: range(n, 2 * n)}[half]:
                    d, a, c = steps[s]
                    last = pe.matmul(bank[:, :], w[name][:, a, d, pair * P:(pair + 1) * P], src[:, c, d, :],
                                     start=s == 0, stop=s == 2 * n - 1)
                if half != 0:
                    last.then_inc(job_full, 1)

            def project_v(b, job):
                g, t = job[-2:]
                bank = job_bank(b, job)
                pe.wait_ge(job_done, job_value(b, job) - 2)
                for d in range(DT):
                    for a, c in PRODUCTS:
                        last = pe.matmul(bank[:, :], inT["ctx"][:, a, d, t * P:(t + 1) * P],
                                         w["v"][:, c, d, g * 512:(g + 1) * 512],
                                         start=d == 0 and (a, c) == (HI, HI), stop=d == DT - 1 and (a, c) == (LO, HI))
                last.then_inc(job_full, 1)

            def scores(b, pair, i):
                if (b is not None) or i > 0:
                    pe.wait_ge(masked, pair_value(b, pair, 8, 2 * i))
                keys = slice(KEYS_OF[i][0] * P, (KEYS_OF[i][-1] + 1) * P)
                n = len(KEYS_OF[i]) * P
                s = pair % 2
                for a, c in PRODUCTS:
                    for h in range(2):
                        rows = slice(h * HEAD, (h + 1) * HEAD)
                        last = pe.matmul(score_ps[h][:, 0:n], qT[rows, s, a, i * P:(i + 1) * P], kT[rows, s, c, keys],
                                         start=(a, c) == (HI, HI), stop=(a, c) == (LO, HI))
                last.then_inc(scored, 1)

            def transposes(b, pair, g):
                first, n, q = GROUPS[g]
                for h in range(2):
                    m = 2 * g + h
                    pe.wait_ge(tr_done, pair_value(b, pair, 6, m + 1))
                    pe.wait_ge(normed, pair_value(b, pair, 8, 2 * q + h + 1))
                    for j in range(n):
                        last = pe.transpose(tr_ps[h][:, j * P:(j + 1) * P],
                                            probs[:, h, (first + j) * P:(first + j + 1) * P], ident[:, :])
                    last.then_inc(tr_full, 1)

            def times_v(b, pair, h):
                pe.wait_ge(pv_done, pair_value(b, pair, 2, h + 1))
                pe.wait_ge(tr_done, pair_value(b, pair, 6, 4 + h + 1) + 2)
                if pair == PAIRS // 2 and h == 0:
                    pe.wait_ge(job_done, job_value(b, v_jobs(1)[-1]))
                head = (2 * pair + h) % VH
                for k in range(TILES):
                    qs = KEYS_OF[k]
                    at = block_of(qs[0], k)
                    span = slice(at, at + 2 * (len(qs) - 1) + 1, 2)
                    assert [block_of(q, k) for q in qs] == [at + 2 * n for n in range(len(qs))]
                    out = out_ps[h][:, qs[0] * P:(qs[-1] + 1) * P]
                    pe.matmul(out.rearrange("p (n m) -> p n m", m=P),
                              v[:, k, head, :, :].rearrange("p a d -> p (a d)"), pT[:, h, HI, span, :],
                              start=k == 0, stop=False, skip_group_check=True)
                    last = pe.matmul(out[0:HEAD].rearrange("p (n m) -> p n m", m=P), v[:, k, head, HI, :], pT[:, h, LO, span, :],
                                     start=False, stop=k == TILES - 1, skip_group_check=True)
                last.then_inc(pv_full, 1)

            pe.wait_ge(const_done, 3)
            for job in INPUT_JOBS:
                input_job(None, job, 0)
            pe.wait_ge(job_done, job_value(None, ("x", 3)))
            pe.wait_ge(w_lo, len(chunks))
            project(None, ("q", 0))
            project(None, ("k", 0))
            for job in v_jobs(0):
                project_v(None, job)
            pe.wait_ge(job_done, job_value(None, ("k", 0)))
            for i in range(TILES):
                scores(None, 0, i)
                if i == 1:
                    project(None, ("q", 1))
                if i == 3:
                    project(None, ("k", 1))

            def batch(b, last):
                for k in range(1, PAIRS + 1):
                    fill = [lambda: None] * 8
                    if k < PAIRS - 1 or (k == PAIRS and not last):
                        pre, pair = ((), k + 1) if k < PAIRS - 1 else (("next",), 1)
                        q, kk = pre + ("q", pair), pre + ("k", pair)
                        fill[0] = lambda: project(b, q, 0)
                        fill[1] = lambda: project(b, q, 1)
                        fill[3] = lambda: project(b, kk, 0)
                        fill[6] = lambda: project(b, kk, 1)
                    elif k == PAIRS - 1 and not last:
                        def inputs(jobs):
                            for job in jobs:
                                input_job(b, ("next",) + job, b + 1)

                        def first_pair():
                            inputs(INPUT_JOBS[6:8])
                            pe.wait_ge(job_done, job_value(b, ("next", "x", 3)))
                            project(b, ("next", "q", 0))
                            project(b, ("next", "k", 0))
                        fill[0] = lambda: inputs(INPUT_JOBS[0:2])
                        fill[1] = lambda: inputs(INPUT_JOBS[2:4])
                        fill[4] = lambda: inputs(INPUT_JOBS[4:6])
                        fill[6] = first_pair
                    transposes(b, k - 1, 0)
                    fill[0]()
                    transposes(b, k - 1, 1)
                    fill[1]()
                    transposes(b, k - 1, 2)
                    with_scores = k < PAIRS or not last
                    if with_scores:
                        pre, pair = ((), k) if k < PAIRS else (("next",), 0)
                        if k > 1:
                            pe.wait_ge(job_done, job_value(b, pre + ("k", pair)))
                        else:
                            pe.wait_ge(job_done, len(LOOP_JOBS) * b + len(HEAD_JOBS))
                        scores(b, k, 0)
                    fill[3]()
                    if with_scores:
                        scores(b, k, 1)
                    fill[4]()
                    times_v(b, k - 1, 0)
                    if with_scores:
                        scores(b, k, 2)
                    times_v(b, k - 1, 1)
                    if with_scores:
                        scores(b, k, 3)
                    fill[6]()
                    if k == PAIRS // 2:
                        for job in v_jobs(1):
                            project_v(b, job)
                    if k == PAIRS and not last:
                        for job in v_jobs(0):
                            project_v(b, ("next",) + job)

            with pe.Fori(0, batches - 1) as b:
                batch(b, False)
            batch(batches - 1, True)

        def job_parts(job):
            kind = [a for a in job if a != "next"]
            if kind[0] in inT:
                t = kind[1]
                dst = [inT[kind[0]][:, a, :, t * P:(t + 1) * P] for a in (HI, LO)]
                return dst, "p (d n) -> p d n", {"d": DT}
            if kind[0] == "v":
                return [v[:, kind[2], :, a, :] for a in (HI, LO)], "p (h d) -> p h d", {"h": VH}
            dst = {"q": qT, "k": kT}[kind[0]]
            return [dst[:, kind[1] % 2, a, :] for a in (HI, LO)], None, {}

        def step_jobs(k, last):
            nxt = [("next",) + j for j in HEAD_JOBS]
            if k < PAIRS - 1:
                out = [[], [("q", k + 1)], [], [], [("k", k + 1)] + (v_jobs(1) if k == PAIRS // 2 else [])]
            elif last:
                out = [[], [], [], [], []]
            elif k == PAIRS - 1:
                out = [nxt[0:2], nxt[2:4], [], nxt[4:6], nxt[6:10]]
            else:
                out = [[], [("next", "q", 1)], [], [], [("next", "k", 1)] + [("next",) + j for j in v_jobs(0)]]
            return out

        @block.scalar
        def _(act):
            def hi_part(b, job):
                dst, view, kw = job_parts(job)
                act.wait_ge(job_full, job_value(b, job))
                act.activation(dst[HI], (job_bank(b, job)[:, :].rearrange(view, **kw) if kw else job_bank(b, job)[:, :]), ACT.Copy).then_inc(job_hi, 1)

            def tr_parts(b, pair, g):
                first, n, _ = GROUPS[g]
                for h in range(2):
                    act.wait_ge(tr_full, pair_value(b, pair, 6, 2 * g + h + 1))
                    act.activation(pT[:, h, HI, first:first + n, :], tr_ps[h][:, 0:n * P].rearrange("p (n m) -> p n m", m=P),
                                   ACT.Copy).then_inc(tr_hi, 1)

            def exps(b, pair, i):
                for h in range(2):
                    c = 2 * i + h
                    act.wait_ge(masked, pair_value(b, pair, 8, c + 1))
                    act.activation(probs[:, h, score_span(i)], probs[:, h, score_span(i)], ACT.Exp,
                                   bias=neg_max[:, c:c + 1], scale=-1.0, accum_out=sums[:, c:c + 1]).then_inc(exped, 1)

            def half(b, pair, h):
                act.wait_ge(pv_full, pair_value(b, pair, 2, h + 1))
                act.wait_ge(pv_done, pair_value(b, pair, 2, h) + 2)
                act.activation(low_half[:, :], out_ps[h][HEAD:P, :], ACT.Copy).then_inc(pv_half, 1)

            for c, (n, d, hf) in enumerate(chunks):
                act.wait_ge(w_loaded[c % 4], 16 * (c // 4 + 1))
                act.activation(w[n][:, HI, d, hf * 512:(hf + 1) * 512], stage[:, c % 4, :], ACT.Copy).then_inc(w_hi, 1)
                if c % 3 == 2:
                    hi_part(None, HEAD_JOBS[c // 3])
            for job in HEAD_JOBS[8:14]:
                hi_part(None, job)
            exps(None, 0, 0)
            exps(None, 0, 1)
            hi_part(None, ("q", 1))
            exps(None, 0, 2)
            exps(None, 0, 3)
            hi_part(None, ("k", 1))

            def batch(b, last):
                for k in range(1, PAIRS + 1):
                    jobs = step_jobs(k, last)
                    with_scores = k < PAIRS or not last
                    for g in range(3):
                        tr_parts(b, k - 1, g)
                        for job in jobs[g]:
                            hi_part(b, job)
                    if with_scores:
                        exps(b, k, 0)
                        exps(b, k, 1)
                    for job in jobs[3]:
                        hi_part(b, job)
                    half(b, k - 1, 0)
                    if with_scores:
                        exps(b, k, 2)
                    half(b, k - 1, 1)
                    if with_scores:
                        exps(b, k, 3)
                    for job in jobs[4]:
                        hi_part(b, job)

            with act.Fori(0, batches - 1) as b:
                batch(b, False)
            batch(batches - 1, True)

        @block.vector
        def _(dve):
            def lo_part(b, job):
                dst, view, kw = job_parts(job)
                dve.wait_ge(job_hi, job_value(b, job))
                dve.tensor_tensor(dst[LO], (job_bank(b, job)[:, :].rearrange(view, **kw) if kw else job_bank(b, job)[:, :]), dst[HI].bitcast(F32),
                                  ALU.subtract).then_inc(job_done, 1)

            def tr_parts(b, pair, g):
                first, n, _ = GROUPS[g]
                for h in range(2):
                    dve.wait_ge(tr_hi, pair_value(b, pair, 6, 2 * g + h + 1))
                    dve.tensor_tensor(pT[:, h, LO, first:first + n, :], tr_ps[h][:, 0:n * P].rearrange("p (n m) -> p n m", m=P),
                                      pT[:, h, HI, first:first + n, :].bitcast(F32), ALU.subtract).then_inc(tr_done, 1)

            def mask(b, pair, i):
                wait_alone(dve, scored, pair_value(b, pair, 4, i + 1), dve_passed)
                n = len(KEYS_OF[i]) * P
                at = (KEYS_OF[i][0] - (i - 1)) * P
                for h in range(2):
                    c = 2 * i + h
                    nc.vector.tensor_tensor_reduce(
                        out=probs[:, h, score_span(i)], in0=score_ps[h][:, 0:n], in1=band[:, at:at + n],
                        scale=-(HEAD ** -0.5), scalar=LARGEST, op0=ALU.add, op1=ALU.min,
                        accum_out=neg_max[:, c:c + 1]).then_inc(masked, 1)

            def invert(b, pair, i):
                dve.wait_ge(exped, pair_value(b, pair, 8, 2 * i + 2))
                dve.reciprocal(inv_sums[:, 2 * i:2 * i + 2], sums[:, 2 * i:2 * i + 2]).then_inc(inverted, 1)

            def add_halves(b, pair, h):
                if h == 0:
                    n = pair // 2 if b is None else PAIRS // 2 * b + pair // 2
                    dve.wait_ge(stored[pair % 2], 16 * n + 16)
                dve.wait_ge(pv_half, pair_value(b, pair, 2, h + 1))
                dve.tensor_tensor(out_sb[h * HEAD:(h + 1) * HEAD, pair % 2, :], out_ps[h][0:HEAD, :], low_half[:, :],
                                  ALU.add).then_inc(pv_done, 1)

            def ln_stats(b, two):
                base = 10 * b + 5 * two
                tiles = (2 * two, 2 * two + 1)
                for t in tiles:
                    dve.wait_ge(in_loaded["x"][t % 2], 32 * b + 16 * (two + 1))
                    dve.bn_stats(stats[:, t, :], raw["x"][:, t % 2, :]).then_inc(ln_step, 1)
                for n, t in enumerate(tiles):
                    wait_alone(dve, ln_step, base + n + 1, dve_passed)
                    dve.bn_aggr(mean_var[:, t, :], stats[:, t, :]).then_inc(ln_step, 1)
                dve.wait_ge(ln_step, base + 4)
                dve.tensor_scalar(var_eps[:, tiles[0]:tiles[1] + 1], mean_var[:, tiles[0]:tiles[1] + 1, 1], EPS, None,
                                  ALU.add).then_inc(ln_step, 1)

            def ln_apply(b, two):
                dve.wait_ge(rstd_ready, 2 * b + two + 1)
                for t in (2 * two, 2 * two + 1):
                    dve.tensor_scalar(raw["x"][:, t % 2, :], raw["x"][:, t % 2, :], mean_var[:, t, 0:1], rstd[:, t:t + 1],
                                      ALU.subtract, ALU.mult).then_inc(x_normed, 1)

            dve.wait_ge(const_done, 3)
            for s in (tr_done, pv_done):
                dve.sem_inc(s, 2)
            ln_stats(0, 0)
            ln_apply(0, 0)
            for c, (n, d, hf) in enumerate(chunks):
                dve.wait_ge(w_hi, c + 1)
                part = w[n][:, :, d, hf * 512:(hf + 1) * 512]
                dve.tensor_tensor(part[:, LO, :], stage[:, c % 4, :], part[:, HI, :].bitcast(F32),
                                  ALU.subtract).then_inc(w_lo, 1)
                if c % 3 == 2:
                    if c // 3 == 5:
                        ln_stats(0, 1)
                        ln_apply(0, 1)
                    lo_part(None, HEAD_JOBS[c // 3])
            for job in HEAD_JOBS[8:14]:
                lo_part(None, job)
            mask(None, 0, 0)
            mask(None, 0, 1)
            invert(None, 0, 0)
            lo_part(None, ("q", 1))
            mask(None, 0, 2)
            invert(None, 0, 1)
            mask(None, 0, 3)
            invert(None, 0, 2)
            invert(None, 0, 3)
            lo_part(None, ("k", 1))

            def batch(b, last):
                for k in range(1, PAIRS + 1):
                    jobs = step_jobs(k, last)
                    with_scores = k < PAIRS or not last
                    if k == PAIRS - 2 and not last:
                        ln_stats(b + 1, 0)
                    for g in range(3):
                        tr_parts(b, k - 1, g)
                        for job in jobs[g]:
                            lo_part(b, job)
                    if k == PAIRS - 2 and not last:
                        ln_apply(b + 1, 0)
                    if with_scores:
                        mask(b, k, 0)
                        mask(b, k, 1)
                        invert(b, k, 0)
                    for job in jobs[3]:
                        lo_part(b, job)
                    if k == PAIRS - 1 and not last:
                        ln_stats(b + 1, 1)
                    if with_scores:
                        mask(b, k, 2)
                        invert(b, k, 1)
                    add_halves(b, k - 1, 0)
                    if with_scores:
                        mask(b, k, 3)
                        invert(b, k, 2)
                    if k == PAIRS - 1 and not last:
                        ln_apply(b + 1, 1)
                    add_halves(b, k - 1, 1)
                    if with_scores:
                        invert(b, k, 3)
                    for job in jobs[4]:
                        lo_part(b, job)

            with dve.Fori(0, batches - 1) as b:
                batch(b, False)
            batch(batches - 1, True)

        @block.gpsimd
        def _(pool):
            pool.memset(minus_half[:, :], -0.5).then_inc(filled, 1)
            pool.memset(ident[:, :], 0.0).then_inc(filled, 1)
            pool.memset(band[:, :], 0.0).then_inc(filled, 1)
            pool.wait_ge(filled, 3)

            def rstds(b, two):
                pool.wait_ge(ln_step, 10 * b + 5 * two + 5)
                pool.tensor_tensor(out=rstd[:, 2 * two:2 * two + 2], in0=var_eps[:, 2 * two:2 * two + 2],
                                   in1=minus_half[:, :], op=ALU.pow).then_inc(rstd_ready, 1)

            def normalise(b, pair, i):
                wait_alone(pool, inverted, pair_value(b, pair, 4, i + 1), pool_passed)
                for h in range(2):
                    c = 2 * i + h
                    pool.tensor_scalar(probs[:, h, score_span(i)], probs[:, h, score_span(i)], inv_sums[:, c:c + 1], 1.0,
                                       ALU.mult, ALU.mult).then_inc(normed, 1)

            pool.affine_select(out=ident[:, :], in_=ident[:, :], compare_op=ALU.not_equal, fill=1.0, base=0,
                               pattern=[[-1, P]], channel_multiplier=1).then_inc(const_done, 1)
            pool.affine_select(out=band[:, 0:P], in_=band[:, 0:P], compare_op=ALU.is_ge, fill=MASKED,
                               base=WINDOW - P, pattern=[[1, P]], channel_multiplier=-1).then_inc(const_done, 1)
            pool.affine_select(out=band[:, 2 * P:], in_=band[:, 2 * P:], compare_op=ALU.is_ge, fill=MASKED,
                               base=WINDOW - P, pattern=[[-1, P]], channel_multiplier=1).then_inc(const_done, 1)
            rstds(0, 0)
            rstds(0, 1)
            for i in range(TILES):
                normalise(None, 0, i)

            def batch(b, last):
                for k in range(1, PAIRS + 1):
                    if k == PAIRS - 2 and not last:
                        rstds(b + 1, 0)
                    for i in range(TILES):
                        if k < PAIRS or not last:
                            normalise(b, k, i)
                        if k == PAIRS - 1 and i == 1 and not last:
                            rstds(b + 1, 1)

            with pool.Fori(0, batches - 1) as b:
                batch(b, False)
            batch(batches - 1, True)


def channel_mix(nc, x, heads_in, wo, w_r, w_k, w_v, mu_r, mu_k, g_attn, g_mix, out):
    batches = x.shape[0]
    D = x.shape[3]
    DT = D // P
    ET = wo.shape[0]
    N = TILES * P
    assert batches % 2 == 0 and batches >= 4 and DT == TILES

    with ExitStack() as es:
        def sb(name, shape, dt=F32):
            return es.enter_context(nc.sbuf_tensor(name, shape, dt))

        def ps(name, shape):
            return es.enter_context(nc.psum_tensor(name, shape, F32))

        def sem(name):
            return es.enter_context(nc.semaphore(name))

        wo_p = sb("wo_parts", [P, 2, ET, D], F32R)
        wT = {n: sb(f"w{n}T", [P, 2, DT, D], F32R) for n in "krv"}
        heads_raw = sb("heads_raw", [P, 2, ET, P])
        heads_p = sb("heads_parts", [P, 2, 2, ET, P], F32R)
        x1 = sb("x1", [P, 2, TILES, D])
        xn = sb("xn", [P, TILES, D])
        xnT = sb("xnT", [P, DT, N + 2])
        mixT = {n: sb(f"mix_{n}T", [P, 2, DT, N], F32R) for n in "kr"}
        shifted = sb("shifted", [P, 2, N])
        mixed = sb("mixed", [P, 2, N])
        relu = sb("relu", [P, 2, N])
        actT = sb("actT", [P, 2, DT, N], F32R)
        gate = sb("gate", [P, TILES, D])
        mu = {n: sb(f"mu_{n}_col", [P, DT]) for n in "kr"}
        one_minus_mu = {n: sb(f"one_minus_mu_{n}", [P, DT]) for n in "kr"}
        tanh_g = sb("tanh_g", [P, 2])
        ident = sb("ident2", [P, P])
        minus_half = sb("minus_half2", [P, 1])
        stats = sb("stats2", [P, TILES, 6])
        mean_var = sb("mean_var2", [P, TILES, 2])
        var_eps = sb("var_eps2", [P, TILES])
        rstd = sb("rstd2", [P, TILES])

        proj_ps = [ps(f"proj{i}", [P, 512]) for i in range(2)]
        tr_ps = [ps(f"tr2_{i}", [P, 512]) for i in range(2)]
        mix_ps = [ps(f"mix{i}", [P, 512]) for i in range(TILES)]

        dve_passed = sem("dve_passed2")
        pool_passed = sem("pool_passed2")
        filled = sem("filled2")
        const_done = sem("const_done2")
        small_loaded = sem("small_loaded")
        small_done = sem("small_done")
        tanh_done = sem("tanh_done")
        w_loaded = [sem(f"w_loaded2_{i}") for i in range(4)]
        w_turned = sem("w_turned")
        w_hi = sem("w_hi2")
        w_lo = sem("w_lo2")
        heads_loaded = [sem(f"heads_loaded{i}") for i in range(2)]
        heads_hi = sem("heads_hi")
        heads_lo = sem("heads_lo")
        x_loaded = [sem(f"x_loaded{i}") for i in range(2)]
        proj_full = sem("proj_full")
        x1_ready = sem("x1_ready")
        ln_step = sem("ln_step2")
        rstd_ready = sem("rstd_ready2")
        xn_ready = sem("xn_ready")
        tr_full = sem("tr_full2")
        tr_done = sem("tr_done2")
        shift_ready = sem("shift_ready")
        mix_ready = sem("mix_ready")
        mix_hi = sem("mix_hi")
        mix_lo = sem("mix_lo")
        k_full = sem("k_full")
        relu_done = sem("relu_done")
        squared = sem("squared")
        act_hi = sem("act_hi")
        act_lo = sem("act_lo")
        r_full = sem("r_full")
        gate_done = sem("gate_done")
        v_full = sem("v_full")
        gated = sem("gated")
        finished = sem("finished")
        stored = [sem(f"stored2_{i}") for i in range(2)]

        chunks = [("o", e) for e in range(ET)] + [(n, d) for n in "krv" for d in range(DT)]
        MIXES = [(n, d) for n in "kr" for d in range(DT)]

        def split_chunk(c):
            n, i = chunks[c]
            if n == "o":
                return [wo_p[:, a, i, :] for a in (HI, LO)]
            return [wT[n][:, a, :, i * P:(i + 1) * P] for a in (HI, LO)]

        def chunk_source(c):
            if chunks[c][0] == "o":
                return xn[:, c % 4, :]
            return tr_ps[c % 2][:, :].rearrange("p (d n) -> p d n", n=P)

        def all_batches(eng, batch):
            with eng.Fori(0, batches // 2 - 1) as two:
                for parity in range(2):
                    batch(two, parity, True, True)
            batch(batches // 2 - 1, 0, True, False)
            batch(batches // 2 - 1, 1, False, False)

        block = es.enter_context(nc.Block())

        @block.sync
        def _(sp):
            def load_heads(b, t):
                if not (isinstance(b, int) and TILES * b + t < 2):
                    sp.wait_ge(heads_lo, TILES * b + (t - 1))
                sp.dma_start(heads_raw[:, t % 2, :, :], heads_in[b, t]).then_inc(heads_loaded[t % 2], 16)

            def load_x(b, parity):
                sp.dma_start(x1[:, parity, :, :], x[b].rearrange("t p n -> p t n")).then_inc(x_loaded[parity], 16)

            with nc.allow_non_contiguous_dma(reason="512 mixing factors onto partitions, once"):
                sp.dma_start(mu["k"][:, :], mu_k.rearrange("(c p) -> p c", p=P)).then_inc(small_loaded, 16)
                sp.dma_start(mu["r"][:, :], mu_r.rearrange("(c p) -> p c", p=P)).then_inc(small_loaded, 16)
            for i, g in enumerate((g_attn, g_mix)):
                sp.dma_start(tanh_g[:, i:i + 1], g.rearrange("(a n) -> a n", a=1).to_broadcast([P, 1])).then_inc(small_loaded, 16)
            for c, (n, i) in enumerate(chunks):
                if c >= 4:
                    m = c - 4
                    if chunks[m][0] == "o":
                        sp.wait_ge(w_lo, m + 1)
                    else:
                        sp.wait_ge(w_turned, m + 1 - ET)
                src = wo[i] if n == "o" else {"k": w_k, "r": w_r, "v": w_v}[n][i]
                sp.dma_start(xn[:, c % 4, :], src).then_inc(w_loaded[c % 4], 16)
                if c == ET - 1:
                    load_heads(0, 0)
                    load_heads(0, 1)
                    load_x(0, 0)
            for b, t in ((0, 2), (0, 3), (1, 0), (1, 1)):
                load_heads(b, t)
            for n in stored:
                sp.sem_inc(n, 16 * TILES)

            def batch(two, parity, has_next, has_second):
                b = 2 * two + parity
                if has_next:
                    sp.wait_ge(stored[1 - parity], 16 * TILES * two + 16 * TILES * (parity + 1))
                    load_x(b + 1, 1 - parity)
                    load_heads(b + 1, 2)
                    load_heads(b + 1, 3)
                if has_second:
                    load_heads(b + 2, 0)
                    load_heads(b + 2, 1)
                for t in range(TILES):
                    sp.wait_ge(finished, TILES * b + (t + 1))
                    sp.dma_start(out[b, t], x1[:, parity, t, :]).then_inc(stored[parity], 16)

            all_batches(sp, batch)
            for s in stored:
                sp.wait_ge(s, 16 * TILES * (batches // 2 + 1))

        @block.tensor
        def _(pe):
            def products(bank, left, right, count):
                n = 0
                for i in range(count):
                    for a, c in PRODUCTS:
                        last = pe.matmul(bank[:, :], left(a, i), right(c, i), start=n == 0, stop=n == 3 * count - 1)
                        n += 1
                return last

            def project(b, t):
                pe.wait_ge(heads_lo, TILES * b + (t + 1))
                if not (isinstance(b, int) and TILES * b + t < 2):
                    pe.wait_ge(x1_ready, TILES * b + (t - 1))
                products(proj_ps[t % 2], lambda a, i: heads_p[:, t % 2, a, i, :], lambda c, i: wo_p[:, c, i, :],
                         ET).then_inc(proj_full, 1)

            def turn(b, t):
                pe.wait_ge(xn_ready, TILES * b + (t + 1))
                if not (isinstance(b, int) and TILES * b + t < 2):
                    pe.wait_ge(tr_done, TILES * b + (t - 1))
                for d in range(DT):
                    last = pe.transpose(tr_ps[t % 2][:, d * P:(d + 1) * P], xn[:, t, d * P:(d + 1) * P], ident[:, :])
                last.then_inc(tr_full, 1)

            def k_product(b, c):
                if c == 0:
                    pe.wait_ge(mix_lo, 2 * TILES * b + TILES)
                pe.wait_ge(gated, TILES * b + (c + 1))
                products(mix_ps[c], lambda a, i: wT["k"][:, a, i, c * P:(c + 1) * P], lambda e, i: mixT["k"][:, e, i, :],
                         DT).then_inc(k_full, 1)

            def r_product(b, t):
                if t == 0:
                    pe.wait_ge(mix_lo, 2 * TILES * b + 2 * TILES)
                pe.wait_ge(relu_done, TILES * b + (t + 1))
                products(mix_ps[t], lambda a, i: mixT["r"][:, a, i, t * P:(t + 1) * P], lambda e, i: wT["r"][:, e, i, :],
                         DT).then_inc(r_full, 1)

            def v_product(b, t):
                if t == 0:
                    pe.wait_ge(act_lo, TILES * b + (TILES + 2))
                pe.wait_ge(gate_done, TILES * b + (t + 1))
                products(mix_ps[t], lambda a, i: actT[:, a, i, t * P:(t + 1) * P], lambda e, i: wT["v"][:, e, i, :],
                         DT).then_inc(v_full, 1)

            pe.wait_ge(const_done, 1)
            for c in range(ET, len(chunks)):
                pe.wait_ge(w_loaded[c % 4], 16 * (c // 4 + 1))
                if c - ET >= 2:
                    pe.wait_ge(w_lo, c - 1)
                for d in range(DT):
                    last = pe.transpose(tr_ps[c % 2][:, d * P:(d + 1) * P], xn[:, c % 4, d * P:(d + 1) * P], ident[:, :])
                last.then_inc(w_turned, 1)
            pe.wait_ge(w_lo, len(chunks))
            for t in range(TILES):
                project(0, t)
            for t in range(TILES):
                turn(0, t)

            def batch(two, parity, has_next, has_second):
                b = 2 * two + parity
                for t in range(TILES):
                    k_product(b, t)
                    if has_next:
                        project(b + 1, t)
                for t in range(TILES):
                    r_product(b, t)
                if has_next:
                    for t in range(TILES):
                        turn(b + 1, t)
                for t in range(TILES):
                    v_product(b, t)

            all_batches(pe, batch)

        @block.scalar
        def _(act):
            def heads_part(b, t):
                act.wait_ge(heads_loaded[t % 2], 16 * (TILES // 2) * b + 16 * (t // 2 + 1))
                if not (isinstance(b, int) and TILES * b + t < 2):
                    act.wait_ge(proj_full, TILES * b + (t - 1))
                act.activation(heads_p[:, t % 2, HI, :, :], heads_raw[:, t % 2, :, :], ACT.Copy).then_inc(heads_hi, 1)

            def turned(b, t):
                act.wait_ge(tr_full, TILES * b + (t + 1))
                act.activation(xnT[:, :, 1 + t * P:1 + (t + 1) * P], tr_ps[t % 2][:, :].rearrange("p (d n) -> p d n", n=P),
                               ACT.Copy).then_inc(tr_done, 1)

            def mix_part(b, m):
                n, d = MIXES[m]
                act.wait_ge(mix_ready, 2 * TILES * b + (m + 1))
                act.activation(mixT[n][:, HI, d, :], mixed[:, m % 2, :], ACT.Copy).then_inc(mix_hi, 1)

            def relu_k(b, c):
                act.wait_ge(k_full, TILES * b + (c + 1))
                act.wait_ge(act_lo, TILES * b + (c + 1))
                act.activation(relu[:, c % 2, :], mix_ps[c][:, :], ACT.Relu).then_inc(relu_done, 1)

            def act_part(b, c):
                act.wait_ge(squared, TILES * b + (c + 1))
                act.activation(actT[:, HI, c, :], relu[:, c % 2, :], ACT.Copy).then_inc(act_hi, 1)

            def gate_r(b, t):
                act.wait_ge(r_full, TILES * b + (t + 1))
                act.activation(gate[:, t, :], mix_ps[t][:, :], ACT.Sigmoid).then_inc(gate_done, 1)

            act.wait_ge(small_loaded, 64)
            act.activation(tanh_g[:, :], tanh_g[:, :], ACT.Tanh).then_inc(tanh_done, 1)
            for c in range(len(chunks)):
                if c < ET:
                    act.wait_ge(w_loaded[c % 4], 16 * (c // 4 + 1))
                else:
                    act.wait_ge(w_turned, c - ET + 1)
                act.activation(split_chunk(c)[HI], chunk_source(c), ACT.Copy).then_inc(w_hi, 1)
                if c in (ET, ET + 2):
                    heads_part(0, (c - ET) // 2)
            for t in range(2, TILES):
                heads_part(0, t)
            for t in range(TILES):
                turned(0, t)
            for m in range(2 * TILES):
                mix_part(0, m)
            for t in range(2):
                heads_part(1, t)

            def batch(two, parity, has_next, has_second):
                b = 2 * two + parity
                relu_k(b, 0)
                act_part(b, 0)
                relu_k(b, 1)
                if has_next:
                    heads_part(b + 1, 2)
                act_part(b, 1)
                relu_k(b, 2)
                if has_next:
                    heads_part(b + 1, 3)
                act_part(b, 2)
                relu_k(b, 3)
                act_part(b, 3)
                for t in range(TILES):
                    gate_r(b, t)
                if has_next:
                    for t in range(TILES):
                        turned(b + 1, t)
                    for m in range(2 * TILES):
                        mix_part(b + 1, m)
                if has_second:
                    heads_part(b + 2, 0)
                    heads_part(b + 2, 1)

            all_batches(act, batch)

        @block.vector
        def _(dve):
            def residual(b, parity, t):
                if t == 0:
                    dve.wait_ge(x_loaded[parity], x_loads(b, parity))
                dve.wait_ge(proj_full, TILES * b + (t + 1))
                dve.scalar_tensor_tensor(out=x1[:, parity, t, :], in0=proj_ps[t % 2][:, :], scalar=tanh_g[:, 0:1],
                                         in1=x1[:, parity, t, :], op0=ALU.mult, op1=ALU.add).then_inc(x1_ready, 1)

            def statistics(b, parity, t):
                n = 3 * TILES * b
                dve.wait_ge(x1_ready, TILES * b + (t + 1))
                dve.bn_stats(stats[:, t, :], x1[:, parity, t, :]).then_inc(ln_step, 1)
                wait_alone(dve, ln_step, n + (3 * t + 1), dve_passed)
                dve.bn_aggr(mean_var[:, t, :], stats[:, t, :]).then_inc(ln_step, 1)
                dve.wait_ge(ln_step, n + (3 * t + 2))
                dve.tensor_scalar(var_eps[:, t:t + 1], mean_var[:, t, 1:2], EPS, None, ALU.add).then_inc(ln_step, 1)

            def normalise(b, parity, t):
                dve.wait_ge(rstd_ready, TILES * b + (t + 1))
                dve.tensor_scalar(xn[:, t, :], x1[:, parity, t, :], mean_var[:, t, 0:1], rstd[:, t:t + 1],
                                  ALU.subtract, ALU.mult).then_inc(xn_ready, 1)

            def mix(b, m):
                n, d = MIXES[m]
                dve.wait_ge(shift_ready, 2 * TILES * b + (m + 1))
                if not (isinstance(b, int) and b == 0 and m < 2):
                    dve.wait_ge(mix_lo, 2 * TILES * b + (m - 1))
                dve.scalar_tensor_tensor(out=mixed[:, m % 2, :], in0=xnT[:, d, 1:N + 1], scalar=mu[n][:, d:d + 1],
                                         in1=shifted[:, m % 2, :], op0=ALU.mult, op1=ALU.add).then_inc(mix_ready, 1)

            def mix_part(b, m):
                n, d = MIXES[m]
                dve.wait_ge(mix_hi, 2 * TILES * b + (m + 1))
                dve.tensor_tensor(mixT[n][:, LO, d, :], mixed[:, m % 2, :], mixT[n][:, HI, d, :].bitcast(F32),
                                  ALU.subtract).then_inc(mix_lo, 1)

            def square(b, c):
                dve.wait_ge(relu_done, TILES * b + (c + 1))
                dve.tensor_tensor(relu[:, c % 2, :], relu[:, c % 2, :], relu[:, c % 2, :], ALU.mult).then_inc(squared, 1)

            def act_part(b, c):
                dve.wait_ge(act_hi, TILES * b + (c + 1))
                dve.tensor_tensor(actT[:, LO, c, :], relu[:, c % 2, :], actT[:, HI, c, :].bitcast(F32),
                                  ALU.subtract).then_inc(act_lo, 1)

            def gate_v(b, t):
                dve.wait_ge(v_full, TILES * b + (t + 1))
                dve.tensor_tensor(gate[:, t, :], mix_ps[t][:, :], gate[:, t, :], ALU.mult).then_inc(gated, 1)

            def finish(b, parity, t):
                dve.wait_ge(gated, TILES * b + (t + 1 + TILES))
                dve.scalar_tensor_tensor(out=x1[:, parity, t, :], in0=gate[:, t, :], scalar=tanh_g[:, 1:2],
                                         in1=x1[:, parity, t, :], op0=ALU.mult, op1=ALU.add).then_inc(finished, 1)

            def x_loads(b, parity):
                return 16 * ((b - parity) // 2 + 1) if isinstance(b, int) else 8 * b + (16 - 8 * parity)

            dve.memset(xnT[:, :, 0:1], 0.0).then_inc(small_done, 1)
            dve.wait_ge(small_loaded, 64)
            for n in "kr":
                dve.tensor_scalar(one_minus_mu[n][:, :], mu[n][:, :], -1.0, 1.0, ALU.mult, ALU.add).then_inc(small_done, 1)
            dve.sem_inc(act_lo, 2)
            dve.sem_inc(gated, TILES)
            for c in range(len(chunks)):
                dve.wait_ge(w_hi, c + 1)
                hi, lo = split_chunk(c)
                dve.tensor_tensor(lo, chunk_source(c), hi.bitcast(F32), ALU.subtract).then_inc(w_lo, 1)
            dve.wait_ge(tanh_done, 1)
            for t in range(TILES):
                residual(0, 0, t)
                statistics(0, 0, t)
            for t in range(TILES):
                normalise(0, 0, t)
            for m in range(2 * TILES):
                mix(0, m)
                if m >= 1:
                    mix_part(0, m - 1)
            mix_part(0, 2 * TILES - 1)

            def batch(two, parity, has_next, has_second):
                b = 2 * two + parity
                for t in range(TILES):
                    square(b, t)
                    if has_next and t >= 1:
                        normalise(b + 1, 1 - parity, t - 1)
                    act_part(b, t)
                    if has_next:
                        residual(b + 1, 1 - parity, t)
                        statistics(b + 1, 1 - parity, t)
                if has_next:
                    normalise(b + 1, 1 - parity, TILES - 1)
                    for m in range(TILES):
                        mix(b + 1, m)
                        if m >= 1:
                            mix_part(b + 1, m - 1)
                for t in range(TILES):
                    if has_next:
                        mix(b + 1, TILES + t)
                        mix_part(b + 1, TILES + t - 1)
                    gate_v(b, t)
                    finish(b, parity, t)
                if has_next:
                    mix_part(b + 1, 2 * TILES - 1)

            all_batches(dve, batch)

        @block.gpsimd
        def _(pool):
            def heads_part(b, t):
                pool.wait_ge(heads_hi, TILES * b + (t + 1))
                pool.tensor_tensor(out=heads_p[:, t % 2, LO, :, :], in0=heads_raw[:, t % 2, :, :],
                                   in1=heads_p[:, t % 2, HI, :, :].bitcast(F32), op=ALU.subtract).then_inc(heads_lo, 1)

            def rstds(b, t):
                pool.wait_ge(ln_step, 3 * TILES * b + 3 * (t + 1))
                pool.tensor_tensor(out=rstd[:, t:t + 1], in0=var_eps[:, t:t + 1], in1=minus_half[:, :],
                                   op=ALU.pow).then_inc(rstd_ready, 1)

            def shift(b, m):
                n, d = MIXES[m]
                if m == 0:
                    wait_alone(pool, tr_done, TILES * b + TILES, pool_passed)
                if not (isinstance(b, int) and b == 0 and m < 2):
                    wait_alone(pool, mix_ready, 2 * TILES * b + (m - 1), pool_passed)
                pool.tensor_scalar(shifted[:, m % 2, :], xnT[:, d, 0:N], one_minus_mu[n][:, d:d + 1], 1.0,
                                   ALU.mult, ALU.mult).then_inc(shift_ready, 1)

            pool.memset(minus_half[:, :], -0.5).then_inc(filled, 1)
            pool.memset(ident[:, :], 0.0).then_inc(filled, 1)
            pool.wait_ge(filled, 2)
            pool.affine_select(out=ident[:, :], in_=ident[:, :], compare_op=ALU.not_equal, fill=1.0, base=0,
                               pattern=[[-1, P]], channel_multiplier=1).then_inc(const_done, 1)
            for t in range(TILES):
                heads_part(0, t)
            for t in range(TILES):
                rstds(0, t)
            pool.wait_ge(small_done, 3)
            for m in range(2 * TILES):
                shift(0, m)
            heads_part(1, 0)
            heads_part(1, 1)

            def batch(two, parity, has_next, has_second):
                b = 2 * two + parity
                if has_next:
                    rstds(b + 1, 0)
                    heads_part(b + 1, 2)
                    rstds(b + 1, 1)
                    heads_part(b + 1, 3)
                    rstds(b + 1, 2)
                    rstds(b + 1, 3)
                    for m in range(2 * TILES):
                        shift(b + 1, m)
                if has_second:
                    heads_part(b + 2, 0)
                    heads_part(b + 2, 1)

            all_batches(pool, batch)


def build(nc, x, ctx_in, g_attn, g_mix, wq, wk, wv, wo, w_r, w_k, w_v, mu_r, mu_k, out):
    batches, S, D = x.shape
    E = wq.shape[1]
    assert S == TILES * P and E == 2 * HEAD * PAIRS
    heads = nc.dram_tensor("heads", (batches, TILES, P, PAIRS, P), F32, kind="Internal").ap()

    def tiled(a):
        return a.rearrange("b (t p) n -> b t p n", p=P)

    def rows(a):
        return a.rearrange("(t p) n -> t p n", p=P)

    attention(nc, tiled(x), tiled(ctx_in), rows(wq), rows(wk), rows(wv), heads)
    channel_mix(nc, tiled(x), heads, rows(wo), rows(w_r), rows(w_k), rows(w_v), mu_r, mu_k, g_attn, g_mix, tiled(out))


INPUTS = ["x", "ctx_1024", "g_xattn", "g_ffn", "L0_xattn_Wq", "L0_xattn_Wk", "L0_xattn_Wv", "L0_xattn_Wo",
          "L0_ffn_W_r", "L0_ffn_W_k", "L0_ffn_W_v", "L0_ffn_mu_r", "L0_ffn_mu_k"]


def kernel(**inputs):
    import numpy as np
    import concourse.bacc as bacc
    from concourse.bass_utils import run_bass_kernel_spmd

    nc = bacc.Bacc("TRN2", target_bir_lowering=False, num_devices=1)
    arrays, args = {}, []
    for name in INPUTS:
        a = np.ascontiguousarray(inputs[name])
        arrays[f"in_{name}"] = a
        args.append(nc.dram_tensor(f"in_{name}", a.shape, mybir.dt.from_np(a.dtype), kind="ExternalInput").ap())
    out = nc.dram_tensor("out_x", arrays["in_x"].shape, F32, kind="ExternalOutput").ap()
    build(nc, *args, out)
    result = run_bass_kernel_spmd(nc, [arrays], core_ids=[0])
    return result.results[0]["out_x"]
```

```python
from contextlib import ExitStack

import concourse.bass as bass
from concourse import mybir

F32 = mybir.dt.float32
F32R = mybir.dt.float32r
ALU = mybir.AluOpType
ACT = mybir.ActivationFunctionType

P = 128
HEAD = 64
WINDOW = 128
EPS = 1e-5
MASKED = -1e30
LARGEST = 3e38
HI, LO = 0, 1
PRODUCTS = ((HI, HI), (HI, LO), (LO, HI))

TILES = 4
KEYS_OF = [range(max(i - 1, 0), min(i + 2, TILES)) for i in range(TILES)]
FIRST = [sum(len(KEYS_OF[a]) for a in range(i)) for i in range(TILES)]
BLOCKS = sum(len(k) for k in KEYS_OF)
GROUPS = [(0, 4, 1), (4, 4, 2), (8, 2, 3)]


def wait_alone(eng, sem, value, passed):
    eng.wait_ge(sem, value)
    eng.sem_inc(passed, 1)


def block_of(q, k):
    return FIRST[q] + k - KEYS_OF[q][0]


PAIRS = 8
INPUT_JOBS = [("ctx", 0), ("ctx", 1), ("x", 0), ("x", 1), ("ctx", 2), ("ctx", 3), ("x", 2), ("x", 3)]


def qk_jobs(pair):
    return [("q", pair), ("k", pair)]


def v_jobs(group):
    return [("v", group, t) for t in range(TILES)]


HEAD_JOBS = INPUT_JOBS + qk_jobs(0) + qk_jobs(1) + v_jobs(0)
OWN_JOBS = (qk_jobs(2) + qk_jobs(3) + qk_jobs(4) + qk_jobs(5) + v_jobs(1) + qk_jobs(6)
            + [("k", PAIRS - 1), ("q", PAIRS - 1)])
NEXT_JOBS = ([("ctx", t) for t in range(TILES)] + [("x", 0), ("x", 1), ("k", 0), ("x", 2), ("x", 3), ("q", 0)]
             + qk_jobs(1) + v_jobs(0))
LOOP_JOBS = OWN_JOBS + [("next",) + j for j in NEXT_JOBS]


def step(k, last):
    jobs = [[] for _ in range(9)]

    def nxt(*names):
        return [(("next",) + name, None) for name in names]

    if k < PAIRS - 2 or (k == PAIRS and not last):
        pre, pair = ((), k + 1) if k < PAIRS else (("next",), 1)
        q, kk = pre + ("q", pair), pre + ("k", pair)
        jobs[0], jobs[2], jobs[4], jobs[6] = [(q, 0)], [(q, 1)], [(kk, 0)], [(kk, 1)]
        if k == PAIRS // 2:
            jobs[8] = [(job, None) for job in v_jobs(1)]
        if k == PAIRS:
            jobs[8] = nxt(*v_jobs(0))
    elif k == PAIRS - 2:
        q, kk = ("q", PAIRS - 1), ("k", PAIRS - 1)
        jobs[0], jobs[2], jobs[4], jobs[6] = [(kk, 0)], [(kk, 1)], [(q, 0)], [(q, 1)]
        if not last:
            jobs[7], jobs[8] = nxt(("ctx", 0)), nxt(("ctx", 1))
    elif k == PAIRS - 1 and not last:
        kk = ("next", "k", 0)
        jobs[0], jobs[2], jobs[4], jobs[5] = nxt(("ctx", 2)), nxt(("ctx", 3), ("x", 0)), nxt(("x", 1)), [(kk, 0)]
        jobs[6], jobs[7], jobs[8] = [(kk, 1)], nxt(("x", 2)), nxt(("x", 3), ("q", 0))
    order = [("turn", 0), ("scores", 0), ("turn", 1), ("scores", 1), ("turn", 2), ("scores", 2), ("values", 0),
             ("scores", 3), ("values", 1)]
    behind = {0: 0, 2: 2, 4: 4, 5: 5, 6: 6, 7: 7, 8: 8}
    units = []
    for n, unit in enumerate(order):
        if unit[0] != "scores" or k < PAIRS or not last:
            units.append(unit)
        units += [("job", job, half) for job, half in jobs[behind[n]]] if n in behind else []
    return units


def attention(nc, x, ctx_in, wq, wk, wv, heads_out):
    batches = x.shape[0]
    D = x.shape[3]
    E = wq.shape[2]
    DT = D // P
    VH = D // HEAD
    assert E == PAIRS * P and DT == TILES and VH == 8

    with ExitStack() as es:
        def sb(name, shape, dt=F32):
            return es.enter_context(nc.sbuf_tensor(name, shape, dt))

        def ps(name, shape):
            return es.enter_context(nc.psum_tensor(name, shape, F32))

        def sem(name):
            return es.enter_context(nc.semaphore(name))

        w = {n: sb(f"w{n}_parts", [P, 2, DT, E], F32R) for n in "qkv"}
        inT = {n: sb(f"{n}T", [P, 2, DT, TILES * P], F32R) for n in ("ctx", "x")}
        qT = sb("qT", [P, 2, 2, TILES * P], F32R)
        kT = sb("kT", [P, 2, 2, TILES * P], F32R)
        v = sb("v", [P, TILES, VH, 2, HEAD], F32R)
        raw = {n: sb(f"raw_{n}", [P, 2, D]) for n in ("ctx", "x")}
        probs = sb("probs", [P, 2, BLOCKS * P])
        pT = sb("pT", [P, 2, 2, BLOCKS, P], F32R)
        low_half = sb("low_half", [HEAD, TILES * P])
        out_sb = sb("out_sb", [P, 2, TILES * P])
        band = sb("band", [P, 3 * P])
        ident = sb("ident", [P, P])
        neg_max = sb("neg_max", [P, 8])
        sums = sb("sums", [P, 8])
        inv_sums = sb("inv_sums", [P, 8])
        stats = sb("stats", [P, TILES, 6])
        mean_var = sb("mean_var", [P, TILES, 2])
        var_eps = sb("var_eps", [P, TILES])
        rstd = sb("rstd", [P, TILES])
        minus_half = sb("minus_half", [P, 2])

        job_ps = [ps(f"job{i}", [P, 512]) for i in range(2)]
        score_ps = [ps(f"score{i}", [P, 512]) for i in range(2)]
        tr_ps = [ps(f"tr{i}", [P, 512]) for i in range(2)]
        out_ps = [ps(f"out{i}", [P, 512]) for i in range(2)]

        dve_passed = sem("dve_passed")
        pool_passed = sem("pool_passed")
        filled = sem("filled")
        const_done = sem("const_done")
        w_loaded = [sem(f"w_loaded{i}") for i in range(4)]
        w_hi = sem("w_hi")
        w_lo = sem("w_lo")
        in_loaded = {n: [sem(f"{n}_loaded{i}") for i in range(2)] for n in ("ctx", "x")}
        ln_step = sem("ln_step")
        rstd_ready = sem("rstd_ready")
        x_normed = sem("x_normed")
        job_full = sem("job_full")
        job_hi = sem("job_hi")
        job_done = sem("job_done")
        scored = sem("scored")
        masked = sem("masked")
        exped = sem("exped")
        inverted = sem("inverted")
        normed = sem("normed")
        tr_full = sem("tr_full")
        tr_hi = sem("tr_hi")
        tr_done = sem("tr_done")
        pv_full = sem("pv_full")
        pv_half = sem("pv_half")
        pv_done = sem("pv_done")
        stored = [sem(f"stored{i}") for i in range(2)]

        def job_value(b, job):
            if b is None:
                return HEAD_JOBS.index(job) + 1
            return len(LOOP_JOBS) * b + (len(HEAD_JOBS) + LOOP_JOBS.index(job) + 1)

        def job_bank(b, job):
            n = HEAD_JOBS.index(job) if b is None else len(HEAD_JOBS) + LOOP_JOBS.index(job)
            return job_ps[n % 2]

        def pair_value(b, pair, per, n):
            return per * PAIRS * b + (per * pair + n) if b is not None else per * pair + n

        def score_span(i):
            return slice(FIRST[i] * P, (FIRST[i] + len(KEYS_OF[i])) * P)

        chunks = [(n, d, half) for half in range(E // 512) for n in "qkv" for d in range(DT)]
        stage = probs[:, :, :].rearrange("p h n -> p (h n)")[:, 0:4 * 512].rearrange("p (s n) -> p s n", s=4)

        block = es.enter_context(nc.Block())

        @block.sync
        def _(sp):
            def load(b, name, t):
                src = (ctx_in if name == "ctx" else x)[b, t]
                sp.dma_start(raw[name][:, t % 2, :], src).then_inc(in_loaded[name][t % 2], 16)

            def load_second(name, b_jobs, b, prefix):
                for t in (2, 3):
                    sp.wait_ge(job_full, job_value(b_jobs, prefix + (name, t - 2)))
                    load(b, name, t)

            for name, t in INPUT_JOBS[:4]:
                load(0, name, t)
            for c, (n, d, half) in enumerate(chunks):
                if c >= 4:
                    sp.wait_ge(w_lo, c - 3)
                src = {"q": wq, "k": wk, "v": wv}[n][d, :, half * 512:(half + 1) * 512]
                sp.dma_start(stage[:, c % 4, :], src).then_inc(w_loaded[c % 4], 16)
                if c == 7:
                    load_second("ctx", None, 0, ())
                    load_second("x", None, 0, ())
            for s in stored:
                sp.sem_inc(s, 16)

            def store(b, pair):
                sp.wait_ge(pv_done, pair_value(b, pair, 2, 2) + 2)
                sp.dma_start(heads_out[b, :, :, pair, :].rearrange("t p n -> p t n"),
                             out_sb[:, pair % 2, :].rearrange("p (t n) -> p t n", n=P)).then_inc(stored[pair % 2], 16)

            def batch(b, last):
                if not last:
                    for name, t in INPUT_JOBS[:4]:
                        sp.wait_ge(job_full, len(LOOP_JOBS) * b + (len(HEAD_JOBS) - len(NEXT_JOBS) + NEXT_JOBS.index(("x", 3)) + 1))
                        load(b + 1, name, t)
                for pair in range(PAIRS):
                    if pair == PAIRS - 3 and not last:
                        load_second("ctx", b, b + 1, ("next",))
                    if pair == PAIRS - 2 and not last:
                        load_second("x", b, b + 1, ("next",))
                    store(b, pair)

            with sp.Fori(0, batches - 1) as b:
                batch(b, False)
            batch(batches - 1, True)
            for s in stored:
                sp.wait_ge(s, 16 * (1 + batches * PAIRS // 2))

        @block.tensor
        def _(pe):
            def input_job(b, job, src_b):
                name, t = job[-2:]
                value = job_value(b, job)
                bank = job_bank(b, job)
                if b is not None or HEAD_JOBS.index(job) >= 2:
                    pe.wait_ge(job_done, value - 2)
                if name == "ctx":
                    pe.wait_ge(in_loaded["ctx"][t % 2], 32 * src_b + 16 * (t // 2 + 1))
                else:
                    pe.wait_ge(x_normed, TILES * src_b + t + 1)
                for d in range(DT):
                    last = pe.transpose(bank[:, d * P:(d + 1) * P], raw[name][:, t % 2, d * P:(d + 1) * P], ident[:, :])
                last.then_inc(job_full, 1)

            def project(b, job, half=None):
                name, pair = job[-2:]
                bank = job_bank(b, job)
                if half != 1:
                    pe.wait_ge(job_done, job_value(b, job) - 2)
                src = inT["x" if name == "q" else "ctx"]
                steps = [(d, a, c) for d in range(DT) for a, c in PRODUCTS]
                n = len(steps) // 2
                for s in {None: range(2 * n), 0: range(n), 1: range(n, 2 * n)}[half]:
                    d, a, c = steps[s]
                    last = pe.matmul(bank[:, :], w[name][:, a, d, pair * P:(pair + 1) * P], src[:, c, d, :],
                                     start=s == 0, stop=s == 2 * n - 1)
                if half != 0:
                    last.then_inc(job_full, 1)

            def project_v(b, job):
                g, t = job[-2:]
                bank = job_bank(b, job)
                pe.wait_ge(job_done, job_value(b, job) - 2)
                for d in range(DT):
                    for a, c in PRODUCTS:
                        last = pe.matmul(bank[:, :], inT["ctx"][:, a, d, t * P:(t + 1) * P],
                                         w["v"][:, c, d, g * 512:(g + 1) * 512],
                                         start=d == 0 and (a, c) == (HI, HI), stop=d == DT - 1 and (a, c) == (LO, HI))
                last.then_inc(job_full, 1)

            def scores(b, pair, i):
                if (b is not None) or i > 0:
                    pe.wait_ge(masked, pair_value(b, pair, 8, 2 * i))
                keys = slice(KEYS_OF[i][0] * P, (KEYS_OF[i][-1] + 1) * P)
                n = len(KEYS_OF[i]) * P
                s = pair % 2
                for a, c in PRODUCTS:
                    for h in range(2):
                        rows = slice(h * HEAD, (h + 1) * HEAD)
                        last = pe.matmul(score_ps[h][:, 0:n], qT[rows, s, a, i * P:(i + 1) * P], kT[rows, s, c, keys],
                                         start=(a, c) == (HI, HI), stop=(a, c) == (LO, HI))
                last.then_inc(scored, 1)

            def transposes(b, pair, g):
                first, n, q = GROUPS[g]
                for h in range(2):
                    m = 2 * g + h
                    pe.wait_ge(tr_done, pair_value(b, pair, 6, m + 1))
                    pe.wait_ge(normed, pair_value(b, pair, 8, 2 * q + h + 1))
                    for j in range(n):
                        last = pe.transpose(tr_ps[h][:, j * P:(j + 1) * P],
                                            probs[:, h, (first + j) * P:(first + j + 1) * P], ident[:, :])
                    last.then_inc(tr_full, 1)

            def times_v(b, pair, h):
                pe.wait_ge(pv_done, pair_value(b, pair, 2, h + 1))
                pe.wait_ge(tr_done, pair_value(b, pair, 6, 4 + h + 1) + 2)
                if pair == 0 and h == 0:
                    pe.wait_ge(job_done, len(LOOP_JOBS) * b + len(HEAD_JOBS))
                if pair == PAIRS // 2 and h == 0:
                    pe.wait_ge(job_done, job_value(b, v_jobs(1)[-1]))
                head = (2 * pair + h) % VH
                for k in range(TILES):
                    qs = KEYS_OF[k]
                    at = block_of(qs[0], k)
                    span = slice(at, at + 2 * (len(qs) - 1) + 1, 2)
                    assert [block_of(q, k) for q in qs] == [at + 2 * n for n in range(len(qs))]
                    out = out_ps[h][:, qs[0] * P:(qs[-1] + 1) * P]
                    pe.matmul(out.rearrange("p (n m) -> p n m", m=P),
                              v[:, k, head, :, :].rearrange("p a d -> p (a d)"), pT[:, h, HI, span, :],
                              start=k == 0, stop=False, skip_group_check=True)
                    last = pe.matmul(out[0:HEAD].rearrange("p (n m) -> p n m", m=P), v[:, k, head, HI, :], pT[:, h, LO, span, :],
                                     start=False, stop=k == TILES - 1, skip_group_check=True)
                last.then_inc(pv_full, 1)

            pe.wait_ge(const_done, 3)
            for job in INPUT_JOBS:
                input_job(None, job, 0)
            pe.wait_ge(job_done, job_value(None, ("x", 3)))
            pe.wait_ge(w_lo, len(chunks) // 2)
            project(None, ("q", 0))
            project(None, ("k", 0))
            pe.wait_ge(job_done, job_value(None, ("k", 0)))
            scores(None, 0, 0)
            project(None, ("q", 1))
            scores(None, 0, 1)
            project(None, ("k", 1))
            scores(None, 0, 2)
            project_v(None, v_jobs(0)[0])
            scores(None, 0, 3)
            for job in v_jobs(0)[1:]:
                project_v(None, job)
            pe.wait_ge(w_lo, len(chunks))

            def batch(b, last):
                for k in range(1, PAIRS + 1):
                    for kind, what, *half in step(k, last):
                        if kind == "turn":
                            transposes(b, k - 1, what)
                        elif kind == "values":
                            times_v(b, k - 1, what)
                        elif kind == "scores":
                            if what == 0 and k == 1:
                                pe.wait_ge(job_done, len(LOOP_JOBS) * b + (len(HEAD_JOBS) - TILES))
                            elif what == 0:
                                pre, pair = ((), k) if k < PAIRS else (("next",), 0)
                                later = max((pre + ("q", pair), pre + ("k", pair)), key=LOOP_JOBS.index)
                                pe.wait_ge(job_done, job_value(b, later))
                            scores(b, k, what)
                        elif what[-2] in inT:
                            input_job(b, what, b + 1)
                        elif what[-2] in ("q", "k"):
                            if what == ("next", "q", 0):
                                pe.wait_ge(job_done, job_value(b, ("next", "x", 3)))
                            if what == ("next", "k", 0) and half[0] == 0:
                                pe.wait_ge(job_done, job_value(b, ("next", "ctx", 3)))
                            project(b, what, half[0])
                        else:
                            project_v(b, what)

            with pe.Fori(0, batches - 1) as b:
                batch(b, False)
            batch(batches - 1, True)

        def job_parts(job):
            kind = [a for a in job if a != "next"]
            if kind[0] in inT:
                t = kind[1]
                dst = [inT[kind[0]][:, a, :, t * P:(t + 1) * P] for a in (HI, LO)]
                return dst, "p (d n) -> p d n", {"d": DT}
            if kind[0] == "v":
                return [v[:, kind[2], :, a, :] for a in (HI, LO)], "p (h d) -> p h d", {"h": VH}
            dst = {"q": qT, "k": kT}[kind[0]]
            return [dst[:, kind[1] % 2, a, :] for a in (HI, LO)], None, {}

        @block.scalar
        def _(act):
            def hi_part(b, job):
                dst, view, kw = job_parts(job)
                act.wait_ge(job_full, job_value(b, job))
                act.activation(dst[HI], (job_bank(b, job)[:, :].rearrange(view, **kw) if kw else job_bank(b, job)[:, :]), ACT.Copy).then_inc(job_hi, 1)

            def tr_parts(b, pair, g):
                first, n, _ = GROUPS[g]
                for h in range(2):
                    act.wait_ge(tr_full, pair_value(b, pair, 6, 2 * g + h + 1))
                    act.activation(pT[:, h, HI, first:first + n, :], tr_ps[h][:, 0:n * P].rearrange("p (n m) -> p n m", m=P),
                                   ACT.Copy).then_inc(tr_hi, 1)

            def exps(b, pair, i):
                for h in range(2):
                    c = 2 * i + h
                    act.wait_ge(masked, pair_value(b, pair, 8, c + 1))
                    act.activation(probs[:, h, score_span(i)], probs[:, h, score_span(i)], ACT.Exp,
                                   bias=neg_max[:, c:c + 1], scale=-1.0, accum_out=sums[:, c:c + 1]).then_inc(exped, 1)

            def half(b, pair, h):
                act.wait_ge(pv_full, pair_value(b, pair, 2, h + 1))
                act.wait_ge(pv_done, pair_value(b, pair, 2, h) + 2)
                act.activation(low_half[:, :], out_ps[h][HEAD:P, :], ACT.Copy).then_inc(pv_half, 1)

            for c, (n, d, hf) in enumerate(chunks):
                act.wait_ge(w_loaded[c % 4], 16 * (c // 4 + 1))
                act.activation(w[n][:, HI, d, hf * 512:(hf + 1) * 512], stage[:, c % 4, :], ACT.Copy).then_inc(w_hi, 1)
                if c < len(chunks) // 2 and c >= 4:
                    hi_part(None, HEAD_JOBS[c - 4])
                if c == len(chunks) // 2 + 3:
                    hi_part(None, ("q", 0))
                    hi_part(None, ("k", 0))
                if c == len(chunks) // 2 + 7:
                    hi_part(None, ("q", 1))
            exps(None, 0, 0)
            exps(None, 0, 1)
            hi_part(None, ("k", 1))
            exps(None, 0, 2)
            hi_part(None, v_jobs(0)[0])
            exps(None, 0, 3)
            for job in v_jobs(0)[1:]:
                hi_part(None, job)

            def kept(k):
                return k in (PAIRS // 2, PAIRS)

            def batch(b, last):
                for k in range(1, PAIRS + 1):
                    units = step(k, last)
                    for n, (kind, what, *half_of) in enumerate(units):
                        if kind == "turn":
                            tr_parts(b, k - 1, what)
                        elif kind == "values":
                            half(b, k - 1, what)
                        elif kind == "job" and half_of[0] != 0:
                            hi_part(b, what)
                        if n > 0 and units[n - 1][0] == "scores" and units[n - 1][1] < TILES - 1:
                            exps(b, k, units[n - 1][1])
                        if kept(k) and kind == "values" and what == 1 and (k < PAIRS or not last):
                            exps(b, k, TILES - 1)
                        if (kind, what) == ("turn", 0) and k > 1 and not kept(k - 1):
                            exps(b, k - 1, TILES - 1)

            with act.Fori(0, batches - 1) as b:
                batch(b, False)
            batch(batches - 1, True)

        @block.vector
        def _(dve):
            def lo_part(b, job):
                dst, view, kw = job_parts(job)
                dve.wait_ge(job_hi, job_value(b, job))
                dve.tensor_tensor(dst[LO], (job_bank(b, job)[:, :].rearrange(view, **kw) if kw else job_bank(b, job)[:, :]), dst[HI].bitcast(F32),
                                  ALU.subtract).then_inc(job_done, 1)

            def tr_parts(b, pair, g):
                first, n, _ = GROUPS[g]
                for h in range(2):
                    dve.wait_ge(tr_hi, pair_value(b, pair, 6, 2 * g + h + 1))
                    dve.tensor_tensor(pT[:, h, LO, first:first + n, :], tr_ps[h][:, 0:n * P].rearrange("p (n m) -> p n m", m=P),
                                      pT[:, h, HI, first:first + n, :].bitcast(F32), ALU.subtract).then_inc(tr_done, 1)

            def mask(b, pair, i):
                wait_alone(dve, scored, pair_value(b, pair, 4, i + 1), dve_passed)
                n = len(KEYS_OF[i]) * P
                at = (KEYS_OF[i][0] - (i - 1)) * P
                for h in range(2):
                    c = 2 * i + h
                    nc.vector.tensor_tensor_reduce(
                        out=probs[:, h, score_span(i)], in0=score_ps[h][:, 0:n], in1=band[:, at:at + n],
                        scale=-(HEAD ** -0.5), scalar=LARGEST, op0=ALU.add, op1=ALU.min,
                        accum_out=neg_max[:, c:c + 1]).then_inc(masked, 1)

            def invert(b, pair, i):
                dve.wait_ge(exped, pair_value(b, pair, 8, 2 * i + 2))
                dve.reciprocal(inv_sums[:, 2 * i:2 * i + 2], sums[:, 2 * i:2 * i + 2]).then_inc(inverted, 1)

            def add_halves(b, pair, h):
                if h == 0:
                    n = pair // 2 if b is None else PAIRS // 2 * b + pair // 2
                    dve.wait_ge(stored[pair % 2], 16 * n + 16)
                dve.wait_ge(pv_half, pair_value(b, pair, 2, h + 1))
                dve.tensor_tensor(out_sb[h * HEAD:(h + 1) * HEAD, pair % 2, :], out_ps[h][0:HEAD, :], low_half[:, :],
                                  ALU.add).then_inc(pv_done, 1)

            def ln_stats(b, two):
                base = 10 * b + 5 * two
                tiles = (2 * two, 2 * two + 1)
                for t in tiles:
                    dve.wait_ge(in_loaded["x"][t % 2], 32 * b + 16 * (two + 1))
                    dve.bn_stats(stats[:, t, :], raw["x"][:, t % 2, :]).then_inc(ln_step, 1)
                for n, t in enumerate(tiles):
                    wait_alone(dve, ln_step, base + n + 1, dve_passed)
                    dve.bn_aggr(mean_var[:, t, :], stats[:, t, :]).then_inc(ln_step, 1)
                dve.wait_ge(ln_step, base + 4)
                dve.tensor_scalar(var_eps[:, tiles[0]:tiles[1] + 1], mean_var[:, tiles[0]:tiles[1] + 1, 1], EPS, None,
                                  ALU.add).then_inc(ln_step, 1)

            def ln_apply(b, two):
                dve.wait_ge(rstd_ready, 2 * b + two + 1)
                for t in (2 * two, 2 * two + 1):
                    dve.tensor_scalar(raw["x"][:, t % 2, :], raw["x"][:, t % 2, :], mean_var[:, t, 0:1], rstd[:, t:t + 1],
                                      ALU.subtract, ALU.mult).then_inc(x_normed, 1)

            dve.wait_ge(const_done, 3)
            for s in (tr_done, pv_done):
                dve.sem_inc(s, 2)
            ln_stats(0, 0)
            ln_apply(0, 0)
            for c, (n, d, hf) in enumerate(chunks):
                dve.wait_ge(w_hi, c + 1)
                part = w[n][:, :, d, hf * 512:(hf + 1) * 512]
                dve.tensor_tensor(part[:, LO, :], stage[:, c % 4, :], part[:, HI, :].bitcast(F32),
                                  ALU.subtract).then_inc(w_lo, 1)
                if c < len(chunks) // 2 and c >= 4:
                    if c == 9:
                        ln_stats(0, 1)
                        ln_apply(0, 1)
                    lo_part(None, HEAD_JOBS[c - 4])
                if c == len(chunks) // 2 + 3:
                    lo_part(None, ("q", 0))
                    lo_part(None, ("k", 0))
                if c == len(chunks) // 2 + 7:
                    lo_part(None, ("q", 1))
            dve.wait_ge(w_lo, len(chunks))
            mask(None, 0, 0)
            mask(None, 0, 1)
            invert(None, 0, 0)
            lo_part(None, ("k", 1))
            mask(None, 0, 2)
            invert(None, 0, 1)
            lo_part(None, v_jobs(0)[0])
            mask(None, 0, 3)
            invert(None, 0, 2)
            for job in v_jobs(0)[1:]:
                lo_part(None, job)

            def batch(b, last):
                for k in range(1, PAIRS + 1):
                    if k == PAIRS - 4 and not last:
                        ln_stats(b + 1, 0)
                    for kind, what, *half in step(k, last):
                        if kind == "turn":
                            tr_parts(b, k - 1, what)
                            if what == 0:
                                invert(b, k - 1, TILES - 1)
                        elif kind == "values":
                            add_halves(b, k - 1, what)
                            if k == PAIRS - 1 and what == 0 and not last:
                                ln_apply(b + 1, 1)
                        elif kind == "job" and half[0] != 0:
                            lo_part(b, what)
                        elif kind == "scores":
                            mask(b, k, what)
                            if what > 0:
                                invert(b, k, what - 1)
                            if k == PAIRS - 1 and what == 2 and not last:
                                ln_stats(b + 1, 1)
                    if k == PAIRS - 4 and not last:
                        ln_apply(b + 1, 0)

            with dve.Fori(0, batches - 1) as b:
                batch(b, False)
            batch(batches - 1, True)

        @block.gpsimd
        def _(pool):
            pool.memset(minus_half[:, :], -0.5).then_inc(filled, 1)
            pool.memset(ident[:, :], 0.0).then_inc(filled, 1)
            pool.memset(band[:, :], 0.0).then_inc(filled, 1)
            pool.wait_ge(filled, 3)

            def rstds(b, two):
                pool.wait_ge(ln_step, 10 * b + 5 * two + 5)
                pool.tensor_tensor(out=rstd[:, 2 * two:2 * two + 2], in0=var_eps[:, 2 * two:2 * two + 2],
                                   in1=minus_half[:, :], op=ALU.pow).then_inc(rstd_ready, 1)

            def normalise(b, pair, i):
                wait_alone(pool, inverted, pair_value(b, pair, 4, i + 1), pool_passed)
                for h in range(2):
                    c = 2 * i + h
                    pool.tensor_scalar(probs[:, h, score_span(i)], probs[:, h, score_span(i)], inv_sums[:, c:c + 1], 1.0,
                                       ALU.mult, ALU.mult).then_inc(normed, 1)

            pool.affine_select(out=ident[:, :], in_=ident[:, :], compare_op=ALU.not_equal, fill=1.0, base=0,
                               pattern=[[-1, P]], channel_multiplier=1).then_inc(const_done, 1)
            pool.affine_select(out=band[:, 0:P], in_=band[:, 0:P], compare_op=ALU.is_ge, fill=MASKED,
                               base=WINDOW - P, pattern=[[1, P]], channel_multiplier=-1).then_inc(const_done, 1)
            pool.affine_select(out=band[:, 2 * P:], in_=band[:, 2 * P:], compare_op=ALU.is_ge, fill=MASKED,
                               base=WINDOW - P, pattern=[[-1, P]], channel_multiplier=1).then_inc(const_done, 1)
            rstds(0, 0)
            rstds(0, 1)
            for i in range(TILES - 1):
                normalise(None, 0, i)

            def batch(b, last):
                for k in range(1, PAIRS + 1):
                    if k == PAIRS - 4 and not last:
                        rstds(b + 1, 0)
                    normalise(b, k - 1, TILES - 1)
                    for i in range(TILES - 1):
                        if k < PAIRS or not last:
                            normalise(b, k, i)
                        if k == PAIRS - 1 and i == 1 and not last:
                            rstds(b + 1, 1)

            with pool.Fori(0, batches - 1) as b:
                batch(b, False)
            batch(batches - 1, True)


def channel_mix(nc, x, heads_in, wo, w_r, w_k, w_v, mu_r, mu_k, g_attn, g_mix, out):
    batches = x.shape[0]
    D = x.shape[3]
    DT = D // P
    ET = wo.shape[0]
    N = TILES * P
    assert batches % 2 == 0 and batches >= 4 and DT == TILES

    with ExitStack() as es:
        def sb(name, shape, dt=F32):
            return es.enter_context(nc.sbuf_tensor(name, shape, dt))

        def ps(name, shape):
            return es.enter_context(nc.psum_tensor(name, shape, F32))

        def sem(name):
            return es.enter_context(nc.semaphore(name))

        wo_p = sb("wo_parts", [P, 2, ET, D], F32R)
        wT = {n: sb(f"w{n}T", [P, 2, DT, D], F32R) for n in "krv"}
        heads_raw = sb("heads_raw", [P, 2, ET, P])
        heads_p = sb("heads_parts", [P, 2, 2, ET, P], F32R)
        x1 = sb("x1", [P, 2, TILES, D])
        xn = sb("xn", [P, TILES, D])
        xnT = sb("xnT", [P, DT, N + 2])
        mixT = {n: sb(f"mix_{n}T", [P, 2, DT, N], F32R) for n in "kr"}
        shifted = sb("shifted", [P, 2, N])
        mixed = sb("mixed", [P, 2, N])
        relu = sb("relu", [P, 2, N])
        actT = sb("actT", [P, 2, DT, N], F32R)
        gate = sb("gate", [P, TILES, D])
        mu = {n: sb(f"mu_{n}_col", [P, DT]) for n in "kr"}
        one_minus_mu = {n: sb(f"one_minus_mu_{n}", [P, DT]) for n in "kr"}
        tanh_g = sb("tanh_g", [P, 2])
        ident = sb("ident2", [P, P])
        minus_half = sb("minus_half2", [P, 1])
        stats = sb("stats2", [P, TILES, 6])
        mean_var = sb("mean_var2", [P, TILES, 2])
        var_eps = sb("var_eps2", [P, TILES])
        rstd = sb("rstd2", [P, TILES])

        proj_ps = [ps(f"proj{i}", [P, 512]) for i in range(2)]
        tr_ps = [ps(f"tr2_{i}", [P, 512]) for i in range(2)]
        mix_ps = [ps(f"mix{i}", [P, 512]) for i in range(TILES)]

        dve_passed = sem("dve_passed2")
        pool_passed = sem("pool_passed2")
        filled = sem("filled2")
        const_done = sem("const_done2")
        small_loaded = sem("small_loaded")
        small_done = sem("small_done")
        tanh_done = sem("tanh_done")
        w_loaded = [sem(f"w_loaded2_{i}") for i in range(4)]
        w_turned = sem("w_turned")
        w_hi = sem("w_hi2")
        w_lo = sem("w_lo2")
        heads_loaded = [sem(f"heads_loaded{i}") for i in range(2)]
        heads_hi = sem("heads_hi")
        heads_lo = sem("heads_lo")
        x_loaded = [sem(f"x_loaded{i}") for i in range(2)]
        proj_full = sem("proj_full")
        x1_ready = sem("x1_ready")
        ln_step = sem("ln_step2")
        rstd_ready = sem("rstd_ready2")
        xn_ready = sem("xn_ready")
        tr_full = sem("tr_full2")
        tr_done = sem("tr_done2")
        shift_ready = sem("shift_ready")
        mix_ready = sem("mix_ready")
        mix_hi = sem("mix_hi")
        mix_lo = sem("mix_lo")
        k_full = sem("k_full")
        relu_done = sem("relu_done")
        squared = sem("squared")
        act_hi = sem("act_hi")
        act_lo = sem("act_lo")
        r_full = sem("r_full")
        gate_done = sem("gate_done")
        v_full = sem("v_full")
        gated = sem("gated")
        finished = sem("finished")
        stored = [sem(f"stored2_{i}") for i in range(2)]

        chunks = [("o", e) for e in range(ET)] + [(n, d) for n in "krv" for d in range(DT)]
        MIXES = [(n, d) for n in "kr" for d in range(DT)]

        def split_chunk(c):
            n, i = chunks[c]
            if n == "o":
                return [wo_p[:, a, i, :] for a in (HI, LO)]
            return [wT[n][:, a, :, i * P:(i + 1) * P] for a in (HI, LO)]

        def chunk_source(c):
            if chunks[c][0] == "o":
                return xn[:, c % 4, :]
            return tr_ps[c % 2][:, :].rearrange("p (d n) -> p d n", n=P)

        def all_batches(eng, batch):
            with eng.Fori(0, batches // 2 - 1) as two:
                for parity in range(2):
                    batch(two, parity, True, True)
            batch(batches // 2 - 1, 0, True, False)
            batch(batches // 2 - 1, 1, False, False)

        block = es.enter_context(nc.Block())

        @block.sync
        def _(sp):
            def load_heads(b, t):
                if not (isinstance(b, int) and TILES * b + t < 2):
                    sp.wait_ge(heads_lo, TILES * b + (t - 1))
                sp.dma_start(heads_raw[:, t % 2, :, :], heads_in[b, t]).then_inc(heads_loaded[t % 2], 16)

            def load_x(b, parity):
                sp.dma_start(x1[:, parity, :, :], x[b].rearrange("t p n -> p t n")).then_inc(x_loaded[parity], 16)

            with nc.allow_non_contiguous_dma(reason="512 mixing factors onto partitions, once"):
                sp.dma_start(mu["k"][:, :], mu_k.rearrange("(c p) -> p c", p=P)).then_inc(small_loaded, 16)
                sp.dma_start(mu["r"][:, :], mu_r.rearrange("(c p) -> p c", p=P)).then_inc(small_loaded, 16)
            for i, g in enumerate((g_attn, g_mix)):
                sp.dma_start(tanh_g[:, i:i + 1], g.rearrange("(a n) -> a n", a=1).to_broadcast([P, 1])).then_inc(small_loaded, 16)
            load_heads(0, 0)
            load_heads(0, 1)
            for c, (n, i) in enumerate(chunks):
                if c >= 4:
                    m = c - 4
                    if chunks[m][0] == "o":
                        sp.wait_ge(w_lo, m + 1)
                    else:
                        sp.wait_ge(w_turned, m + 1 - ET)
                src = wo[i] if n == "o" else {"k": w_k, "r": w_r, "v": w_v}[n][i]
                sp.dma_start(xn[:, c % 4, :], src).then_inc(w_loaded[c % 4], 16)
                if c == ET - 1:
                    load_x(0, 0)
                if c in (ET + 2, ET + 5):
                    load_heads(0, 2 + (c - ET) // 4)
            for b, t in ((1, 0), (1, 1)):
                load_heads(b, t)
            for n in stored:
                sp.sem_inc(n, 16 * TILES)

            def batch(two, parity, has_next, has_second):
                b = 2 * two + parity
                if has_next:
                    sp.wait_ge(stored[1 - parity], 16 * TILES * two + 16 * TILES * (parity + 1))
                    load_x(b + 1, 1 - parity)
                    load_heads(b + 1, 2)
                    load_heads(b + 1, 3)
                if has_second:
                    load_heads(b + 2, 0)
                    load_heads(b + 2, 1)
                for t in range(TILES):
                    sp.wait_ge(finished, TILES * b + (t + 1))
                    sp.dma_start(out[b, t], x1[:, parity, t, :]).then_inc(stored[parity], 16)

            all_batches(sp, batch)
            for s in stored:
                sp.wait_ge(s, 16 * TILES * (batches // 2 + 1))

        @block.tensor
        def _(pe):
            def products(bank, left, right, count):
                n = 0
                for i in range(count):
                    for a, c in PRODUCTS:
                        last = pe.matmul(bank[:, :], left(a, i), right(c, i), start=n == 0, stop=n == 3 * count - 1)
                        n += 1
                return last

            def project(b, t):
                pe.wait_ge(heads_lo, TILES * b + (t + 1))
                if not (isinstance(b, int) and TILES * b + t < 2):
                    pe.wait_ge(x1_ready, TILES * b + (t - 1))
                products(proj_ps[t % 2], lambda a, i: heads_p[:, t % 2, a, i, :], lambda c, i: wo_p[:, c, i, :],
                         ET).then_inc(proj_full, 1)

            def turn(b, t):
                pe.wait_ge(xn_ready, TILES * b + (t + 1))
                if not (isinstance(b, int) and TILES * b + t < 2):
                    pe.wait_ge(tr_done, TILES * b + (t - 1))
                for d in range(DT):
                    last = pe.transpose(tr_ps[t % 2][:, d * P:(d + 1) * P], xn[:, t, d * P:(d + 1) * P], ident[:, :])
                last.then_inc(tr_full, 1)

            def k_product(b, c):
                if c == 0:
                    pe.wait_ge(mix_lo, 2 * TILES * b + TILES)
                pe.wait_ge(gated, TILES * b + (c + 1))
                products(mix_ps[c], lambda a, i: wT["k"][:, a, i, c * P:(c + 1) * P], lambda e, i: mixT["k"][:, e, i, :],
                         DT).then_inc(k_full, 1)

            def r_product(b, t):
                if t == 0:
                    pe.wait_ge(mix_lo, 2 * TILES * b + 2 * TILES)
                pe.wait_ge(relu_done, TILES * b + (t + 1))
                products(mix_ps[t], lambda a, i: mixT["r"][:, a, i, t * P:(t + 1) * P], lambda e, i: wT["r"][:, e, i, :],
                         DT).then_inc(r_full, 1)

            def v_product(b, t):
                if t == 0:
                    pe.wait_ge(act_lo, TILES * b + (TILES + 2))
                pe.wait_ge(gate_done, TILES * b + (t + 1))
                products(mix_ps[t], lambda a, i: actT[:, a, i, t * P:(t + 1) * P], lambda e, i: wT["v"][:, e, i, :],
                         DT).then_inc(v_full, 1)

            def turn_chunk(c):
                pe.wait_ge(w_loaded[c % 4], 16 * (c // 4 + 1))
                if c - ET >= 2:
                    pe.wait_ge(w_lo, c - 1)
                for d in range(DT):
                    last = pe.transpose(tr_ps[c % 2][:, d * P:(d + 1) * P], xn[:, c % 4, d * P:(d + 1) * P], ident[:, :])
                last.then_inc(w_turned, 1)

            pe.wait_ge(const_done, 1)
            pe.wait_ge(w_lo, ET)
            for t in range(TILES):
                project(0, t)
                for c in range(ET + 3 * t, ET + 3 * t + 3):
                    turn_chunk(c)
            pe.wait_ge(w_lo, len(chunks))
            for t in range(TILES):
                turn(0, t)

            def batch(two, parity, has_next, has_second):
                b = 2 * two + parity
                for t in range(TILES):
                    k_product(b, t)
                    if has_next:
                        project(b + 1, t)
                for t in range(TILES):
                    r_product(b, t)
                if has_next:
                    for t in range(TILES):
                        turn(b + 1, t)
                for t in range(TILES):
                    v_product(b, t)

            all_batches(pe, batch)

        @block.scalar
        def _(act):
            def heads_part(b, t):
                act.wait_ge(heads_loaded[t % 2], 16 * (TILES // 2) * b + 16 * (t // 2 + 1))
                if not (isinstance(b, int) and TILES * b + t < 2):
                    act.wait_ge(proj_full, TILES * b + (t - 1))
                act.activation(heads_p[:, t % 2, HI, :, :], heads_raw[:, t % 2, :, :], ACT.Copy).then_inc(heads_hi, 1)

            def turned(b, t):
                act.wait_ge(tr_full, TILES * b + (t + 1))
                act.activation(xnT[:, :, 1 + t * P:1 + (t + 1) * P], tr_ps[t % 2][:, :].rearrange("p (d n) -> p d n", n=P),
                               ACT.Copy).then_inc(tr_done, 1)

            def mix_part(b, m):
                n, d = MIXES[m]
                act.wait_ge(mix_ready, 2 * TILES * b + (m + 1))
                act.activation(mixT[n][:, HI, d, :], mixed[:, m % 2, :], ACT.Copy).then_inc(mix_hi, 1)

            def relu_k(b, c):
                act.wait_ge(k_full, TILES * b + (c + 1))
                act.wait_ge(act_lo, TILES * b + (c + 1))
                act.activation(relu[:, c % 2, :], mix_ps[c][:, :], ACT.Relu).then_inc(relu_done, 1)

            def act_part(b, c):
                act.wait_ge(squared, TILES * b + (c + 1))
                act.activation(actT[:, HI, c, :], relu[:, c % 2, :], ACT.Copy).then_inc(act_hi, 1)

            def gate_r(b, t):
                act.wait_ge(r_full, TILES * b + (t + 1))
                act.activation(gate[:, t, :], mix_ps[t][:, :], ACT.Sigmoid).then_inc(gate_done, 1)

            act.wait_ge(small_loaded, 64)
            act.activation(tanh_g[:, :], tanh_g[:, :], ACT.Tanh).then_inc(tanh_done, 1)
            for c in range(len(chunks)):
                if c < ET:
                    act.wait_ge(w_loaded[c % 4], 16 * (c // 4 + 1))
                else:
                    act.wait_ge(w_turned, c - ET + 1)
                act.activation(split_chunk(c)[HI], chunk_source(c), ACT.Copy).then_inc(w_hi, 1)
                if c in (1, 3, ET + 2, ET + 5):
                    heads_part(0, {1: 0, 3: 1}.get(c, 2 + (c - ET) // 4))
            for t in range(TILES):
                turned(0, t)
            for m in range(2 * TILES):
                mix_part(0, m)
            for t in range(2):
                heads_part(1, t)

            def batch(two, parity, has_next, has_second):
                b = 2 * two + parity
                relu_k(b, 0)
                act_part(b, 0)
                relu_k(b, 1)
                if has_next:
                    heads_part(b + 1, 2)
                act_part(b, 1)
                relu_k(b, 2)
                if has_next:
                    heads_part(b + 1, 3)
                act_part(b, 2)
                relu_k(b, 3)
                act_part(b, 3)
                for t in range(TILES):
                    gate_r(b, t)
                    if has_second and t < 2:
                        heads_part(b + 2, t)
                if has_next:
                    for t in range(TILES):
                        turned(b + 1, t)
                    for m in range(2 * TILES):
                        mix_part(b + 1, m)

            all_batches(act, batch)

        @block.vector
        def _(dve):
            def residual(b, parity, t):
                if t == 0:
                    dve.wait_ge(x_loaded[parity], x_loads(b, parity))
                dve.wait_ge(proj_full, TILES * b + (t + 1))
                dve.scalar_tensor_tensor(out=x1[:, parity, t, :], in0=proj_ps[t % 2][:, :], scalar=tanh_g[:, 0:1],
                                         in1=x1[:, parity, t, :], op0=ALU.mult, op1=ALU.add).then_inc(x1_ready, 1)

            def statistics(b, parity, t):
                n = 3 * TILES * b
                dve.wait_ge(x1_ready, TILES * b + (t + 1))
                dve.bn_stats(stats[:, t, :], x1[:, parity, t, :]).then_inc(ln_step, 1)
                wait_alone(dve, ln_step, n + (3 * t + 1), dve_passed)
                dve.bn_aggr(mean_var[:, t, :], stats[:, t, :]).then_inc(ln_step, 1)
                dve.wait_ge(ln_step, n + (3 * t + 2))
                dve.tensor_scalar(var_eps[:, t:t + 1], mean_var[:, t, 1:2], EPS, None, ALU.add).then_inc(ln_step, 1)

            def normalise(b, parity, t):
                dve.wait_ge(rstd_ready, TILES * b + (t + 1))
                dve.tensor_scalar(xn[:, t, :], x1[:, parity, t, :], mean_var[:, t, 0:1], rstd[:, t:t + 1],
                                  ALU.subtract, ALU.mult).then_inc(xn_ready, 1)

            def mix(b, m):
                n, d = MIXES[m]
                dve.wait_ge(shift_ready, 2 * TILES * b + (m + 1))
                if not (isinstance(b, int) and b == 0 and m < 2):
                    dve.wait_ge(mix_lo, 2 * TILES * b + (m - 1))
                dve.scalar_tensor_tensor(out=mixed[:, m % 2, :], in0=xnT[:, d, 1:N + 1], scalar=mu[n][:, d:d + 1],
                                         in1=shifted[:, m % 2, :], op0=ALU.mult, op1=ALU.add).then_inc(mix_ready, 1)

            def mix_part(b, m):
                n, d = MIXES[m]
                dve.wait_ge(mix_hi, 2 * TILES * b + (m + 1))
                dve.tensor_tensor(mixT[n][:, LO, d, :], mixed[:, m % 2, :], mixT[n][:, HI, d, :].bitcast(F32),
                                  ALU.subtract).then_inc(mix_lo, 1)

            def square(b, c):
                dve.wait_ge(relu_done, TILES * b + (c + 1))
                dve.tensor_tensor(relu[:, c % 2, :], relu[:, c % 2, :], relu[:, c % 2, :], ALU.mult).then_inc(squared, 1)

            def act_part(b, c):
                dve.wait_ge(act_hi, TILES * b + (c + 1))
                dve.tensor_tensor(actT[:, LO, c, :], relu[:, c % 2, :], actT[:, HI, c, :].bitcast(F32),
                                  ALU.subtract).then_inc(act_lo, 1)

            def gate_v(b, t):
                dve.wait_ge(v_full, TILES * b + (t + 1))
                dve.tensor_tensor(gate[:, t, :], mix_ps[t][:, :], gate[:, t, :], ALU.mult).then_inc(gated, 1)

            def finish(b, parity, t):
                dve.wait_ge(gated, TILES * b + (t + 1 + TILES))
                dve.scalar_tensor_tensor(out=x1[:, parity, t, :], in0=gate[:, t, :], scalar=tanh_g[:, 1:2],
                                         in1=x1[:, parity, t, :], op0=ALU.mult, op1=ALU.add).then_inc(finished, 1)

            def x_loads(b, parity):
                return 16 * ((b - parity) // 2 + 1) if isinstance(b, int) else 8 * b + (16 - 8 * parity)

            dve.memset(xnT[:, :, 0:1], 0.0).then_inc(small_done, 1)
            dve.wait_ge(small_loaded, 64)
            for n in "kr":
                dve.tensor_scalar(one_minus_mu[n][:, :], mu[n][:, :], -1.0, 1.0, ALU.mult, ALU.add).then_inc(small_done, 1)
            dve.sem_inc(act_lo, 2)
            dve.sem_inc(gated, TILES)
            for c in range(len(chunks)):
                dve.wait_ge(w_hi, c + 1)
                hi, lo = split_chunk(c)
                dve.tensor_tensor(lo, chunk_source(c), hi.bitcast(F32), ALU.subtract).then_inc(w_lo, 1)
                if c == ET:
                    dve.wait_ge(tanh_done, 1)
                if c in (ET + 2, ET + 5, ET + 8, ET + 11):
                    residual(0, 0, (c - ET) // 3)
                    statistics(0, 0, (c - ET) // 3)
            for t in range(TILES):
                normalise(0, 0, t)
            for m in range(2 * TILES):
                mix(0, m)
                if m >= 1:
                    mix_part(0, m - 1)
            mix_part(0, 2 * TILES - 1)

            def batch(two, parity, has_next, has_second):
                b = 2 * two + parity
                for t in range(TILES):
                    square(b, t)
                    if has_next and t >= 1:
                        normalise(b + 1, 1 - parity, t - 1)
                    act_part(b, t)
                    if has_next:
                        residual(b + 1, 1 - parity, t)
                        statistics(b + 1, 1 - parity, t)
                if has_next:
                    normalise(b + 1, 1 - parity, TILES - 1)
                    for m in range(TILES):
                        mix(b + 1, m)
                        if m >= 1:
                            mix_part(b + 1, m - 1)
                for t in range(TILES):
                    if has_next:
                        mix(b + 1, TILES + t)
                        mix_part(b + 1, TILES + t - 1)
                    gate_v(b, t)
                    finish(b, parity, t)
                if has_next:
                    mix_part(b + 1, 2 * TILES - 1)

            all_batches(dve, batch)

        @block.gpsimd
        def _(pool):
            def heads_part(b, t):
                pool.wait_ge(heads_hi, TILES * b + (t + 1))
                pool.tensor_tensor(out=heads_p[:, t % 2, LO, :, :], in0=heads_raw[:, t % 2, :, :],
                                   in1=heads_p[:, t % 2, HI, :, :].bitcast(F32), op=ALU.subtract).then_inc(heads_lo, 1)

            def rstds(b, t):
                pool.wait_ge(ln_step, 3 * TILES * b + 3 * (t + 1))
                pool.tensor_tensor(out=rstd[:, t:t + 1], in0=var_eps[:, t:t + 1], in1=minus_half[:, :],
                                   op=ALU.pow).then_inc(rstd_ready, 1)

            def shift(b, m):
                n, d = MIXES[m]
                if m == 0:
                    wait_alone(pool, tr_done, TILES * b + TILES, pool_passed)
                if not (isinstance(b, int) and b == 0 and m < 2):
                    wait_alone(pool, mix_ready, 2 * TILES * b + (m - 1), pool_passed)
                pool.tensor_scalar(shifted[:, m % 2, :], xnT[:, d, 0:N], one_minus_mu[n][:, d:d + 1], 1.0,
                                   ALU.mult, ALU.mult).then_inc(shift_ready, 1)

            pool.memset(minus_half[:, :], -0.5).then_inc(filled, 1)
            pool.memset(ident[:, :], 0.0).then_inc(filled, 1)
            pool.wait_ge(filled, 2)
            pool.affine_select(out=ident[:, :], in_=ident[:, :], compare_op=ALU.not_equal, fill=1.0, base=0,
                               pattern=[[-1, P]], channel_multiplier=1).then_inc(const_done, 1)
            for t in range(TILES):
                heads_part(0, t)
            for t in range(TILES):
                rstds(0, t)
            pool.wait_ge(small_done, 3)
            for m in range(2 * TILES):
                shift(0, m)
            heads_part(1, 0)
            heads_part(1, 1)

            def batch(two, parity, has_next, has_second):
                b = 2 * two + parity
                if has_next:
                    rstds(b + 1, 0)
                    heads_part(b + 1, 2)
                    rstds(b + 1, 1)
                    heads_part(b + 1, 3)
                    rstds(b + 1, 2)
                    rstds(b + 1, 3)
                if has_second:
                    heads_part(b + 2, 0)
                    heads_part(b + 2, 1)
                if has_next:
                    for m in range(2 * TILES):
                        shift(b + 1, m)

            all_batches(pool, batch)


def build(nc, x, ctx_in, g_attn, g_mix, wq, wk, wv, wo, w_r, w_k, w_v, mu_r, mu_k, out):
    batches, S, D = x.shape
    E = wq.shape[1]
    assert S == TILES * P and E == 2 * HEAD * PAIRS
    heads = nc.dram_tensor("heads", (batches, TILES, P, PAIRS, P), F32, kind="Internal").ap()

    def tiled(a):
        return a.rearrange("b (t p) n -> b t p n", p=P)

    def rows(a):
        return a.rearrange("(t p) n -> t p n", p=P)

    attention(nc, tiled(x), tiled(ctx_in), rows(wq), rows(wk), rows(wv), heads)
    channel_mix(nc, tiled(x), heads, rows(wo), rows(w_r), rows(w_k), rows(w_v), mu_r, mu_k, g_attn, g_mix, tiled(out))


INPUTS = ["x", "ctx_1024", "g_xattn", "g_ffn", "L0_xattn_Wq", "L0_xattn_Wk", "L0_xattn_Wv", "L0_xattn_Wo",
          "L0_ffn_W_r", "L0_ffn_W_k", "L0_ffn_W_v", "L0_ffn_mu_r", "L0_ffn_mu_k"]


def kernel(**inputs):
    import numpy as np
    import concourse.bacc as bacc
    from concourse.bass_utils import run_bass_kernel_spmd

    nc = bacc.Bacc("TRN2", target_bir_lowering=False, num_devices=1)
    arrays, args = {}, []
    for name in INPUTS:
        a = np.ascontiguousarray(inputs[name])
        arrays[f"in_{name}"] = a
        args.append(nc.dram_tensor(f"in_{name}", a.shape, mybir.dt.from_np(a.dtype), kind="ExternalInput").ap())
    out = nc.dram_tensor("out_x", arrays["in_x"].shape, F32, kind="ExternalOutput").ap()
    build(nc, *args, out)
    result = run_bass_kernel_spmd(nc, [arrays], core_ids=[0])
    return result.results[0]["out_x"]
```

```python
from contextlib import ExitStack

import concourse.bass as bass
from concourse import mybir

F32 = mybir.dt.float32
F32R = mybir.dt.float32r
ALU = mybir.AluOpType
ACT = mybir.ActivationFunctionType

P = 128
HEAD = 64
WINDOW = 128
EPS = 1e-5
MASKED = -1e30
LARGEST = 3e38
HI, LO = 0, 1
PRODUCTS = ((HI, HI), (HI, LO), (LO, HI))

TILES = 4
KEYS_OF = [range(max(i - 1, 0), min(i + 2, TILES)) for i in range(TILES)]
FIRST = [sum(len(KEYS_OF[a]) for a in range(i)) for i in range(TILES)]
BLOCKS = sum(len(k) for k in KEYS_OF)
GROUPS = [(0, 4, 1), (4, 4, 2), (8, 2, 3)]


def wait_alone(eng, sem, value, passed):
    eng.wait_ge(sem, value)
    eng.sem_inc(passed, 1)


def block_of(q, k):
    return FIRST[q] + k - KEYS_OF[q][0]


PAIRS = 8
INPUT_JOBS = [("ctx", 0), ("ctx", 1), ("x", 0), ("x", 1), ("ctx", 2), ("ctx", 3), ("x", 2), ("x", 3)]


def qk_jobs(pair):
    return [("q", pair), ("k", pair)]


def v_jobs(group):
    return [("v", group, t) for t in range(TILES)]


HEAD_JOBS = INPUT_JOBS + qk_jobs(0) + qk_jobs(1) + v_jobs(0)


def step(k, last):
    def nxt(*names):
        return [("job", ("next",) + name, None) for name in names]

    def halves(*job):
        return [[("job", job, half)] for half in range(2)]

    turn, scores = ([[(kind, n)] for n in range(count)] for kind, count in (("turn", 3), ("scores", TILES)))
    values = [[("values", h)] for h in range(2)]
    stats, apply = ([(kind, t) for t in range(TILES)] for kind in ("stats", "apply"))
    if k < PAIRS - 1:
        (qa, qb), (ka, kb) = (halves(name, k + 1) for name in (("k", "q") if k == PAIRS - 2 else ("q", "k")))
        units = turn[0] + qa + scores[0] + turn[1] + qb + scores[1] + turn[2] + ka + scores[2]
        if k < PAIRS - 2:
            units += kb + values[0] + scores[3] + values[1]
        else:
            units += values[0] + kb + scores[3] + nxt(("ctx", 0)) + values[1] + nxt(("ctx", 1))
        if k == PAIRS // 2:
            v0, v1, v2, v3 = [[("job", job, None)] for job in v_jobs(1)]
            units += v0 + stats[0:2] + v1 + v2 + apply[0:2] + v3
    elif k == PAIRS - 1:
        k0a, k0b = halves("next", "k", 0)
        units = (turn[0] + nxt(("x", 0)) + scores[0] + turn[1] + nxt(("ctx", 2)) + scores[1] + nxt(("ctx", 3)) + turn[2]
                 + nxt(("x", 1)) + scores[2] + k0a + stats[2:3] + values[0] + k0b + stats[3:4] + apply[2:3] + scores[3]
                 + values[1] + apply[3:4] + nxt(("x", 2)))
    else:
        v0, v1, v2, v3 = [nxt(job) for job in v_jobs(0)]
        k1a, k1b = halves("next", "k", 1)
        units = (turn[0] + k1a + nxt(("x", 3)) + turn[1] + k1b + nxt(("q", 0)) + turn[2] + nxt(("q", 1)) + values[0]
                 + scores[0] + values[1] + v0 + scores[1] + v1 + scores[2] + v2 + scores[3] + v3)
    if last:
        units = [u for u in units if u[0] not in ("stats", "apply") and not (u[0] == "job" and u[1][0] == "next")
                 and not (u[0] == "scores" and k == PAIRS)]
    return units


LOOP_JOBS = [u[1] for k in range(1, PAIRS + 1) for u in step(k, False) if u[0] == "job" and u[2] != 0]
NEXT_JOBS = [job[1:] for job in LOOP_JOBS if job[0] == "next"]
assert NEXT_JOBS == [job[1:] for job in LOOP_JOBS[-len(NEXT_JOBS):]] and len(NEXT_JOBS) == len(HEAD_JOBS)
assert len(LOOP_JOBS) % 2 == 0 and len(HEAD_JOBS) % 2 == 0
assert HEAD_JOBS[-TILES:] == NEXT_JOBS[-TILES:] == v_jobs(0)


def attention(nc, x, ctx_in, wq, wk, wv, heads_out, staged, staged_loaded, wo):
    batches = x.shape[0]
    D = x.shape[3]
    E = wq.shape[2]
    DT = D // P
    VH = D // HEAD
    assert E == PAIRS * P and DT == TILES and VH == 8

    with ExitStack() as es:
        def sb(name, shape, dt=F32):
            return es.enter_context(nc.sbuf_tensor(name, shape, dt))

        def ps(name, shape):
            return es.enter_context(nc.psum_tensor(name, shape, F32))

        def sem(name):
            return es.enter_context(nc.semaphore(name))

        w = {n: sb(f"w{n}_parts", [P, 2, DT, E], F32R) for n in "qkv"}
        inT = {n: sb(f"{n}T", [P, 2, DT, TILES * P], F32R) for n in ("ctx", "x")}
        qT = sb("qT", [P, 2, 2, TILES * P], F32R)
        kT = sb("kT", [P, 2, 2, TILES * P], F32R)
        v = sb("v", [P, TILES, VH, 2, HEAD], F32R)
        raw = {"ctx": staged[:, 0:2, :], "x": staged[:, 2:4, :]}
        probs = sb("probs", [P, 2, BLOCKS * P])
        pT = sb("pT", [P, 2, 2, BLOCKS, P], F32R)
        low_half = sb("low_half", [HEAD, TILES * P])
        out_sb = sb("out_sb", [P, 2, TILES * P])
        band = sb("band", [P, 3 * P])
        ident = sb("ident", [P, P])
        neg_max = sb("neg_max", [P, 8])
        sums = sb("sums", [P, 8])
        inv_sums = sb("inv_sums", [P, 8])
        stats = sb("stats", [P, TILES, 6])
        mean_var = sb("mean_var", [P, TILES, 2])
        var_eps = sb("var_eps", [P, TILES])
        rstd = sb("rstd", [P, TILES])
        minus_half = sb("minus_half", [P, 1])

        job_ps = [ps(f"job{i}", [P, 512]) for i in range(2)]
        score_ps = [ps(f"score{i}", [P, 512]) for i in range(2)]
        tr_ps = [ps(f"tr{i}", [P, 512]) for i in range(2)]
        out_ps = [ps(f"out{i}", [P, 512]) for i in range(2)]

        dve_passed = sem("dve_passed")
        pool_passed = sem("pool_passed")
        filled = sem("filled")
        const_done = sem("const_done")
        w_loaded = [sem(f"w_loaded{i}") for i in range(4)]
        w_hi = sem("w_hi")
        w_lo = sem("w_lo")
        in_loaded = {n: [sem(f"{n}_loaded{i}") for i in range(2)] for n in ("ctx", "x")}
        ln_step = sem("ln_step")
        rstd_ready = sem("rstd_ready")
        x_normed = sem("x_normed")
        job_full = sem("job_full")
        job_hi = sem("job_hi")
        job_done = sem("job_done")
        scored = sem("scored")
        masked = sem("masked")
        exped = sem("exped")
        inverted = sem("inverted")
        normed = sem("normed")
        tr_full = sem("tr_full")
        tr_hi = sem("tr_hi")
        tr_done = sem("tr_done")
        pv_full = sem("pv_full")
        pv_half = sem("pv_half")
        pv_done = sem("pv_done")
        stored = [sem(f"stored{i}") for i in range(2)]

        def job_value(b, job):
            if b is None:
                return HEAD_JOBS.index(job) + 1
            return len(LOOP_JOBS) * b + (len(HEAD_JOBS) + LOOP_JOBS.index(job) + 1)

        def job_bank(b, job):
            n = HEAD_JOBS.index(job) if b is None else len(HEAD_JOBS) + LOOP_JOBS.index(job)
            return job_ps[n % 2]

        def pair_value(b, pair, per, n):
            return per * PAIRS * b + (per * pair + n) if b is not None else per * pair + n

        def kept(k):
            return k in (PAIRS // 2, PAIRS)

        def score_span(i):
            return slice(FIRST[i] * P, (FIRST[i] + len(KEYS_OF[i])) * P)

        chunks = [(n, d, half) for half in range(E // 512) for n in "qkv" for d in range(DT)]
        stage = probs[:, :, :].rearrange("p h n -> p (h n)")[:, 0:4 * 512].rearrange("p (s n) -> p s n", s=4)

        block = es.enter_context(nc.Block())

        @block.sync
        def _(sp):
            def load(b, name, t):
                src = (ctx_in if name == "ctx" else x)[b, t]
                sp.dma_start(raw[name][:, t % 2, :], src).then_inc(in_loaded[name][t % 2], 16)

            def load_second(name, b_jobs, b, prefix):
                for t in (2, 3):
                    sp.wait_ge(job_full, job_value(b_jobs, prefix + (name, t - 2)))
                    load(b, name, t)

            for name, t in INPUT_JOBS[:4]:
                load(0, name, t)
            for c, (n, d, half) in enumerate(chunks):
                if c >= 4:
                    sp.wait_ge(w_lo, c - 3)
                src = {"q": wq, "k": wk, "v": wv}[n][d, :, half * 512:(half + 1) * 512]
                sp.dma_start(stage[:, c % 4, :], src).then_inc(w_loaded[c % 4], 16)
                if c == 1:
                    load_second("ctx", None, 0, ())
                if c == 3:
                    load_second("x", None, 0, ())
            for s in stored:
                sp.sem_inc(s, 16)

            def store(b, pair):
                sp.wait_ge(pv_done, pair_value(b, pair, 2, 2) + 2)
                sp.dma_start(heads_out[b, :, :, pair, :].rearrange("t p n -> p t n"),
                             out_sb[:, pair % 2, :].rearrange("p (t n) -> p t n", n=P)).then_inc(stored[pair % 2], 16)

            def batch(b, last):
                if not last:
                    for name, t in INPUT_JOBS[:4]:
                        sp.wait_ge(job_full, len(LOOP_JOBS) * b + (len(HEAD_JOBS) - len(NEXT_JOBS) + NEXT_JOBS.index(("x", 3)) + 1))
                        load(b + 1, name, t)
                for pair in range(PAIRS):
                    if pair == PAIRS - 3 and not last:
                        load_second("ctx", b, b + 1, ("next",))
                    if pair == PAIRS - 2 and not last:
                        load_second("x", b, b + 1, ("next",))
                    store(b, pair)

            with sp.Fori(0, batches - 1) as b:
                batch(b, False)
            sp.wait_ge(job_full, len(LOOP_JOBS) * (batches - 1) + len(HEAD_JOBS))
            for c in range(TILES):
                sp.dma_start(staged[:, c, :], wo[c]).then_inc(staged_loaded[c], 16)
            batch(batches - 1, True)
            for s in stored:
                sp.wait_ge(s, 16 * (1 + batches * PAIRS // 2))

        @block.tensor
        def _(pe):
            def input_job(b, job, src_b):
                name, t = job[-2:]
                value = job_value(b, job)
                bank = job_bank(b, job)
                if b is not None or HEAD_JOBS.index(job) >= 2:
                    pe.wait_ge(job_done, value - 2)
                if name == "ctx":
                    pe.wait_ge(in_loaded["ctx"][t % 2], 32 * src_b + 16 * (t // 2 + 1))
                else:
                    pe.wait_ge(x_normed, TILES * src_b + t + 1)
                for d in range(DT):
                    last = pe.transpose(bank[:, d * P:(d + 1) * P], raw[name][:, t % 2, d * P:(d + 1) * P], ident[:, :])
                last.then_inc(job_full, 1)

            def project(b, job, half=None):
                name, pair = job[-2:]
                bank = job_bank(b, job)
                if half != 1:
                    pe.wait_ge(job_done, job_value(b, job) - 2)
                src = inT["x" if name == "q" else "ctx"]
                steps = [(d, a, c) for d in range(DT) for a, c in PRODUCTS]
                n = len(steps) // 2
                for s in {None: range(2 * n), 0: range(n), 1: range(n, 2 * n)}[half]:
                    d, a, c = steps[s]
                    last = pe.matmul(bank[:, :], w[name][:, a, d, pair * P:(pair + 1) * P], src[:, c, d, :],
                                     start=s == 0, stop=s == 2 * n - 1)
                if half != 0:
                    last.then_inc(job_full, 1)

            def project_v(b, job):
                g, t = job[-2:]
                bank = job_bank(b, job)
                pe.wait_ge(job_done, job_value(b, job) - 2)
                for d in range(DT):
                    for a, c in PRODUCTS:
                        last = pe.matmul(bank[:, :], inT["ctx"][:, a, d, t * P:(t + 1) * P],
                                         w["v"][:, c, d, g * 512:(g + 1) * 512],
                                         start=d == 0 and (a, c) == (HI, HI), stop=d == DT - 1 and (a, c) == (LO, HI))
                last.then_inc(job_full, 1)

            def scores(b, pair, i):
                if (b is not None) or i > 0:
                    pe.wait_ge(masked, pair_value(b, pair, 8, 2 * i))
                keys = slice(KEYS_OF[i][0] * P, (KEYS_OF[i][-1] + 1) * P)
                n = len(KEYS_OF[i]) * P
                s = pair % 2
                for a, c in PRODUCTS:
                    for h in range(2):
                        rows = slice(h * HEAD, (h + 1) * HEAD)
                        last = pe.matmul(score_ps[h][:, 0:n], qT[rows, s, a, i * P:(i + 1) * P], kT[rows, s, c, keys],
                                         start=(a, c) == (HI, HI), stop=(a, c) == (LO, HI))
                last.then_inc(scored, 1)

            def transposes(b, pair, g):
                first, n, q = GROUPS[g]
                for h in range(2):
                    m = 2 * g + h
                    pe.wait_ge(tr_done, pair_value(b, pair, 6, m + 1))
                    pe.wait_ge(normed, pair_value(b, pair, 8, 2 * q + h + 1))
                    for j in range(n):
                        last = pe.transpose(tr_ps[h][:, j * P:(j + 1) * P],
                                            probs[:, h, (first + j) * P:(first + j + 1) * P], ident[:, :])
                    last.then_inc(tr_full, 1)

            def times_v(b, pair, h):
                pe.wait_ge(pv_done, pair_value(b, pair, 2, h + 1))
                pe.wait_ge(tr_done, pair_value(b, pair, 6, 4 + h + 1) + 2)
                if pair == 0 and h == 0:
                    pe.wait_ge(job_done, len(LOOP_JOBS) * b + len(HEAD_JOBS))
                if pair == PAIRS // 2 and h == 0:
                    pe.wait_ge(job_done, job_value(b, v_jobs(1)[-1]))
                head = (2 * pair + h) % VH
                for k in range(TILES):
                    qs = KEYS_OF[k]
                    at = block_of(qs[0], k)
                    span = slice(at, at + 2 * (len(qs) - 1) + 1, 2)
                    assert [block_of(q, k) for q in qs] == [at + 2 * n for n in range(len(qs))]
                    out = out_ps[h][:, qs[0] * P:(qs[-1] + 1) * P]
                    pe.matmul(out.rearrange("p (n m) -> p n m", m=P),
                              v[:, k, head, :, :].rearrange("p a d -> p (a d)"), pT[:, h, HI, span, :],
                              start=k == 0, stop=False, skip_group_check=True)
                    last = pe.matmul(out[0:HEAD].rearrange("p (n m) -> p n m", m=P), v[:, k, head, HI, :], pT[:, h, LO, span, :],
                                     start=False, stop=k == TILES - 1, skip_group_check=True)
                last.then_inc(pv_full, 1)

            pe.wait_ge(const_done, 3)
            for job in INPUT_JOBS:
                input_job(None, job, 0)
            pe.wait_ge(job_done, job_value(None, ("x", 3)))
            pe.wait_ge(w_lo, len(chunks) // 2)
            project(None, ("q", 0))
            project(None, ("k", 0))
            project(None, ("q", 1))
            project(None, ("k", 1))
            pe.wait_ge(job_done, job_value(None, ("k", 0)))
            for t in range(TILES):
                scores(None, 0, t)
                project_v(None, v_jobs(0)[t])
            pe.wait_ge(w_lo, len(chunks))

            def batch(b, last):
                for k in range(1, PAIRS + 1):
                    for kind, what, *half in step(k, last):
                        if kind == "turn":
                            transposes(b, k - 1, what)
                        elif kind == "values":
                            times_v(b, k - 1, what)
                        elif kind == "scores":
                            if what == 0 and k == 1:
                                pe.wait_ge(job_done, len(LOOP_JOBS) * b + (len(HEAD_JOBS) - TILES))
                            elif what == 0:
                                pre, pair = ((), k) if k < PAIRS else (("next",), 0)
                                later = max((pre + ("q", pair), pre + ("k", pair)), key=LOOP_JOBS.index)
                                pe.wait_ge(job_done, job_value(b, later))
                            scores(b, k, what)
                        elif kind != "job":
                            pass
                        elif what[-2] in inT:
                            input_job(b, what, b + 1)
                        elif what[-2] in ("q", "k"):
                            if what == ("next", "q", 0) and half[0] != 1:
                                pe.wait_ge(job_done, job_value(b, ("next", "x", 3)))
                            if what == ("next", "k", 0) and half[0] == 0:
                                pe.wait_ge(job_done, job_value(b, ("next", "ctx", 3)))
                            project(b, what, half[0])
                        else:
                            project_v(b, what)

            with pe.Fori(0, batches - 1) as b:
                batch(b, False)
            batch(batches - 1, True)

        def job_parts(job):
            kind = [a for a in job if a != "next"]
            if kind[0] in inT:
                t = kind[1]
                dst = [inT[kind[0]][:, a, :, t * P:(t + 1) * P] for a in (HI, LO)]
                return dst, "p (d n) -> p d n", {"d": DT}
            if kind[0] == "v":
                return [v[:, kind[2], :, a, :] for a in (HI, LO)], "p (h d) -> p h d", {"h": VH}
            dst = {"q": qT, "k": kT}[kind[0]]
            return [dst[:, kind[1] % 2, a, :] for a in (HI, LO)], None, {}

        @block.scalar
        def _(act):
            def hi_part(b, job):
                dst, view, kw = job_parts(job)
                act.wait_ge(job_full, job_value(b, job))
                act.activation(dst[HI], (job_bank(b, job)[:, :].rearrange(view, **kw) if kw else job_bank(b, job)[:, :]), ACT.Copy).then_inc(job_hi, 1)

            def tr_parts(b, pair, g):
                first, n, _ = GROUPS[g]
                for h in range(2):
                    act.wait_ge(tr_full, pair_value(b, pair, 6, 2 * g + h + 1))
                    act.activation(pT[:, h, HI, first:first + n, :], tr_ps[h][:, 0:n * P].rearrange("p (n m) -> p n m", m=P),
                                   ACT.Copy).then_inc(tr_hi, 1)

            def exps(b, pair, i):
                for h in range(2):
                    c = 2 * i + h
                    act.wait_ge(masked, pair_value(b, pair, 8, c + 1))
                    act.activation(probs[:, h, score_span(i)], probs[:, h, score_span(i)], ACT.Exp,
                                   bias=neg_max[:, c:c + 1], scale=-1.0, accum_out=sums[:, c:c + 1]).then_inc(exped, 1)

            def half(b, pair, h):
                act.wait_ge(pv_full, pair_value(b, pair, 2, h + 1))
                act.wait_ge(pv_done, pair_value(b, pair, 2, h) + 2)
                act.activation(low_half[:, :], out_ps[h][HEAD:P, :], ACT.Copy).then_inc(pv_half, 1)

            half_way = len(chunks) // 2
            qk_at = {half_way + 2 + 3 * n: job for n, job in enumerate(qk_jobs(0) + qk_jobs(1))}
            for c, (n, d, hf) in enumerate(chunks):
                if c < len(INPUT_JOBS):
                    hi_part(None, HEAD_JOBS[c])
                act.wait_ge(w_loaded[c % 4], 16 * (c // 4 + 1))
                act.activation(w[n][:, HI, d, hf * 512:(hf + 1) * 512], stage[:, c % 4, :], ACT.Copy).then_inc(w_hi, 1)
                if c in qk_at:
                    hi_part(None, qk_at[c])
            for t in range(TILES):
                exps(None, 0, t)
                hi_part(None, v_jobs(0)[t])

            def batch(b, last):
                for k in range(1, PAIRS + 1):
                    units = step(k, last)
                    for n, (kind, what, *half_of) in enumerate(units):
                        if kind == "turn":
                            tr_parts(b, k - 1, what)
                        elif kind == "values":
                            half(b, k - 1, what)
                        elif kind == "job" and half_of[0] != 0:
                            hi_part(b, what)
                        if n > 0 and units[n - 1][0] == "scores" and units[n - 1][1] < TILES - 1:
                            exps(b, k, units[n - 1][1])
                        if kept(k) and n > 0 and units[n - 1][:2] == ("scores", TILES - 1):
                            exps(b, k, TILES - 1)
                        if (kind, what) == ("turn", 0) and k > 1 and not kept(k - 1):
                            exps(b, k - 1, TILES - 1)

            with act.Fori(0, batches - 1) as b:
                batch(b, False)
            batch(batches - 1, True)

        @block.vector
        def _(dve):
            def lo_part(b, job):
                dst, view, kw = job_parts(job)
                dve.wait_ge(job_hi, job_value(b, job))
                dve.tensor_tensor(dst[LO], (job_bank(b, job)[:, :].rearrange(view, **kw) if kw else job_bank(b, job)[:, :]), dst[HI].bitcast(F32),
                                  ALU.subtract).then_inc(job_done, 1)

            def tr_parts(b, pair, g):
                first, n, _ = GROUPS[g]
                for h in range(2):
                    dve.wait_ge(tr_hi, pair_value(b, pair, 6, 2 * g + h + 1))
                    dve.tensor_tensor(pT[:, h, LO, first:first + n, :], tr_ps[h][:, 0:n * P].rearrange("p (n m) -> p n m", m=P),
                                      pT[:, h, HI, first:first + n, :].bitcast(F32), ALU.subtract).then_inc(tr_done, 1)

            def mask(b, pair, i):
                wait_alone(dve, scored, pair_value(b, pair, 4, i + 1), dve_passed)
                n = len(KEYS_OF[i]) * P
                at = (KEYS_OF[i][0] - (i - 1)) * P
                for h in range(2):
                    c = 2 * i + h
                    nc.vector.tensor_tensor_reduce(
                        out=probs[:, h, score_span(i)], in0=score_ps[h][:, 0:n], in1=band[:, at:at + n],
                        scale=-(HEAD ** -0.5), scalar=LARGEST, op0=ALU.add, op1=ALU.min,
                        accum_out=neg_max[:, c:c + 1]).then_inc(masked, 1)

            def invert(b, pair, i):
                dve.wait_ge(exped, pair_value(b, pair, 8, 2 * i + 2))
                dve.reciprocal(inv_sums[:, 2 * i:2 * i + 2], sums[:, 2 * i:2 * i + 2]).then_inc(inverted, 1)

            def add_halves(b, pair, h):
                if h == 0:
                    n = pair // 2 if b is None else PAIRS // 2 * b + pair // 2
                    dve.wait_ge(stored[pair % 2], 16 * n + 16)
                dve.wait_ge(pv_half, pair_value(b, pair, 2, h + 1))
                dve.tensor_tensor(out_sb[h * HEAD:(h + 1) * HEAD, pair % 2, :], out_ps[h][0:HEAD, :], low_half[:, :],
                                  ALU.add).then_inc(pv_done, 1)

            def ln_stats(b, t):
                base = 3 * TILES * b + 3 * t
                dve.wait_ge(in_loaded["x"][t % 2], 32 * b + 16 * (t // 2 + 1))
                dve.bn_stats(stats[:, t, :], raw["x"][:, t % 2, :]).then_inc(ln_step, 1)
                wait_alone(dve, ln_step, base + 1, dve_passed)
                dve.bn_aggr(mean_var[:, t, :], stats[:, t, :]).then_inc(ln_step, 1)
                dve.wait_ge(ln_step, base + 2)
                dve.tensor_scalar(var_eps[:, t:t + 1], mean_var[:, t, 1:2], EPS, None, ALU.add).then_inc(ln_step, 1)

            def ln_apply(b, t):
                dve.wait_ge(rstd_ready, TILES * b + t + 1)
                dve.tensor_scalar(raw["x"][:, t % 2, :], raw["x"][:, t % 2, :], mean_var[:, t, 0:1], rstd[:, t:t + 1],
                                  ALU.subtract, ALU.mult).then_inc(x_normed, 1)

            dve.wait_ge(const_done, 3)
            for s in (tr_done, pv_done):
                dve.sem_inc(s, 2)
            for t in range(2):
                ln_stats(0, t)
            for t in range(2):
                ln_apply(0, t)
            half_way = len(chunks) // 2
            qk_at = {half_way + 2 + 3 * n: job for n, job in enumerate(qk_jobs(0) + qk_jobs(1))}
            for c, (n, d, hf) in enumerate(chunks):
                if c < len(INPUT_JOBS):
                    if c == 6:
                        for t in (2, 3):
                            ln_stats(0, t)
                        for t in (2, 3):
                            ln_apply(0, t)
                    lo_part(None, HEAD_JOBS[c])
                dve.wait_ge(w_hi, c + 1)
                part = w[n][:, :, d, hf * 512:(hf + 1) * 512]
                dve.tensor_tensor(part[:, LO, :], stage[:, c % 4, :], part[:, HI, :].bitcast(F32),
                                  ALU.subtract).then_inc(w_lo, 1)
                if c in qk_at:
                    lo_part(None, qk_at[c])
            dve.wait_ge(w_lo, len(chunks))
            for t in range(TILES):
                mask(None, 0, t)
                if t > 0:
                    invert(None, 0, t - 1)
                    lo_part(None, v_jobs(0)[t - 1])
            invert(None, 0, TILES - 1)
            lo_part(None, v_jobs(0)[-1])

            def batch(b, last):
                for k in range(1, PAIRS + 1):
                    units = step(k, last)
                    for n, (kind, what, *half) in enumerate(units):
                        if kind == "turn":
                            tr_parts(b, k - 1, what)
                            if what == 0 and k > 1 and not kept(k - 1):
                                invert(b, k - 1, TILES - 1)
                        elif kind == "values":
                            add_halves(b, k - 1, what)
                        elif kind == "job" and half[0] != 0:
                            lo_part(b, what)
                        elif kind == "scores":
                            mask(b, k, what)
                            if what > 0:
                                invert(b, k, what - 1)
                        elif kind == "stats":
                            ln_stats(b + 1, what)
                        elif kind == "apply":
                            ln_apply(b + 1, what)
                        if kept(k) and n > 0 and units[n - 1][:2] == ("scores", TILES - 1):
                            invert(b, k, TILES - 1)

            with dve.Fori(0, batches - 1) as b:
                batch(b, False)
            batch(batches - 1, True)

        @block.gpsimd
        def _(pool):
            pool.memset(minus_half[:, :], -0.5).then_inc(filled, 1)
            pool.memset(ident[:, :], 0.0).then_inc(filled, 1)
            pool.memset(band[:, :], 0.0).then_inc(filled, 1)
            pool.wait_ge(filled, 3)

            def ln_rstd(b, t):
                pool.wait_ge(ln_step, 3 * TILES * b + 3 * (t + 1))
                pool.tensor_tensor(out=rstd[:, t:t + 1], in0=var_eps[:, t:t + 1], in1=minus_half[:, 0:1],
                                   op=ALU.pow).then_inc(rstd_ready, 1)

            def normalise(b, pair, i):
                wait_alone(pool, inverted, pair_value(b, pair, 4, i + 1), pool_passed)
                for h in range(2):
                    c = 2 * i + h
                    pool.tensor_scalar(probs[:, h, score_span(i)], probs[:, h, score_span(i)], inv_sums[:, c:c + 1], 1.0,
                                       ALU.mult, ALU.mult).then_inc(normed, 1)

            pool.affine_select(out=ident[:, :], in_=ident[:, :], compare_op=ALU.not_equal, fill=1.0, base=0,
                               pattern=[[-1, P]], channel_multiplier=1).then_inc(const_done, 1)
            pool.affine_select(out=band[:, 0:P], in_=band[:, 0:P], compare_op=ALU.is_ge, fill=MASKED,
                               base=WINDOW - P, pattern=[[1, P]], channel_multiplier=-1).then_inc(const_done, 1)
            pool.affine_select(out=band[:, 2 * P:], in_=band[:, 2 * P:], compare_op=ALU.is_ge, fill=MASKED,
                               base=WINDOW - P, pattern=[[-1, P]], channel_multiplier=1).then_inc(const_done, 1)
            for t in range(TILES):
                ln_rstd(0, t)
            for i in range(TILES):
                normalise(None, 0, i)

            def batch(b, last):
                for k in range(1, PAIRS + 1):
                    units = step(k, last)
                    for n, (kind, what, *_) in enumerate(units):
                        if kind == "scores" and what > 0:
                            normalise(b, k, what - 1)
                        if kept(k) and n > 0 and units[n - 1][:2] == ("scores", TILES - 1):
                            normalise(b, k, TILES - 1)
                        if (kind, what) == ("turn", 0) and k > 1 and not kept(k - 1):
                            normalise(b, k - 1, TILES - 1)
                        if kind == "stats":
                            ln_rstd(b + 1, what)

            with pool.Fori(0, batches - 1) as b:
                batch(b, False)
            batch(batches - 1, True)


def channel_mix(nc, x, heads_in, wo, w_r, w_k, w_v, mu_r, mu_k, g_attn, g_mix, out, staged, w_loaded):
    batches = x.shape[0]
    D = x.shape[3]
    DT = D // P
    ET = wo.shape[0]
    N = TILES * P
    assert batches % 2 == 0 and batches >= 4 and DT == TILES

    with ExitStack() as es:
        def sb(name, shape, dt=F32):
            return es.enter_context(nc.sbuf_tensor(name, shape, dt))

        def ps(name, shape):
            return es.enter_context(nc.psum_tensor(name, shape, F32))

        def sem(name):
            return es.enter_context(nc.semaphore(name))

        wo_p = sb("wo_parts", [P, 2, ET, D], F32R)
        wT = {n: sb(f"w{n}T", [P, 2, DT, D], F32R) for n in "krv"}
        heads_raw = sb("heads_raw", [P, 2, ET, P])
        heads_p = sb("heads_parts", [P, 2, 2, ET, P], F32R)
        x1 = sb("x1", [P, 2, TILES, D])
        xn = sb("xn", [P, TILES, D])
        xnT = sb("xnT", [P, DT, N + 2])
        mixT = {n: sb(f"mix_{n}T", [P, 2, DT, N], F32R) for n in "kr"}
        shifted = sb("shifted", [P, 2, N])
        mixed = sb("mixed", [P, 2, N])
        relu = sb("relu", [P, 2, N])
        actT = sb("actT", [P, 2, DT, N], F32R)
        gate = staged
        mu = {n: sb(f"mu_{n}_col", [P, DT]) for n in "kr"}
        one_minus_mu = {n: sb(f"one_minus_mu_{n}", [P, DT]) for n in "kr"}
        tanh_g = sb("tanh_g", [P, 2])
        ident = sb("ident2", [P, P])
        minus_half = sb("minus_half2", [P, 1])
        stats = sb("stats2", [P, TILES, 6])
        mean_var = sb("mean_var2", [P, TILES, 2])
        var_eps = sb("var_eps2", [P, TILES])
        rstd = sb("rstd2", [P, TILES])

        proj_ps = [ps(f"proj{i}", [P, 512]) for i in range(2)]
        tr_ps = [ps(f"tr2_{i}", [P, 512]) for i in range(2)]
        mix_ps = [ps(f"mix{i}", [P, 512]) for i in range(TILES)]

        dve_passed = sem("dve_passed2")
        pool_passed = sem("pool_passed2")
        filled = sem("filled2")
        const_done = sem("const_done2")
        small_loaded = sem("small_loaded")
        small_done = sem("small_done")
        tanh_done = sem("tanh_done")
        w_turned = sem("w_turned")
        w_hi = sem("w_hi2")
        w_lo = sem("w_lo2")
        heads_loaded = [sem(f"heads_loaded{i}") for i in range(2)]
        heads_hi = sem("heads_hi")
        heads_lo = sem("heads_lo")
        x_loaded = [sem(f"x_tile_loaded{t}") for t in range(TILES)]
        proj_full = sem("proj_full")
        x1_ready = sem("x1_ready")
        ln_step = sem("ln_step2")
        rstd_ready = sem("rstd_ready2")
        xn_ready = sem("xn_ready")
        tr_full = sem("tr_full2")
        tr_done = sem("tr_done2")
        shift_ready = sem("shift_ready")
        mix_ready = sem("mix_ready")
        mix_hi = sem("mix_hi")
        mix_lo = sem("mix_lo")
        k_full = sem("k_full")
        relu_done = sem("relu_done")
        squared = sem("squared")
        act_hi = sem("act_hi")
        act_lo = sem("act_lo")
        r_full = sem("r_full")
        gate_done = sem("gate_done")
        v_full = sem("v_full")
        gated = sem("gated")
        finished = sem("finished")
        stored = [sem(f"stored2_{i}") for i in range(2)]

        chunks = [("o", e) for e in range(ET)] + [(n, d) for n in "krv" for d in range(DT)]
        EARLY = 8
        MIXES = [(n, d) for n in "kr" for d in range(DT)]

        def split_chunk(c):
            n, i = chunks[c]
            if n == "o":
                return [wo_p[:, a, i, :] for a in (HI, LO)]
            return [wT[n][:, a, :, i * P:(i + 1) * P] for a in (HI, LO)]

        def chunk_source(c):
            if chunks[c][0] == "o":
                return staged[:, c % 4, :]
            return tr_ps[c % 2][:, :].rearrange("p (d n) -> p d n", n=P)

        def all_batches(eng, batch):
            with eng.Fori(0, batches // 2 - 1) as two:
                for parity in range(2):
                    batch(two, parity, True, True)
            batch(batches // 2 - 1, 0, True, False)
            batch(batches // 2 - 1, 1, False, False)

        block = es.enter_context(nc.Block())

        @block.sync
        def _(sp):
            def load_heads(b, t):
                if not (isinstance(b, int) and TILES * b + t < 2):
                    sp.wait_ge(heads_lo, TILES * b + (t - 1))
                sp.dma_start(heads_raw[:, t % 2, :, :], heads_in[b, t]).then_inc(heads_loaded[t % 2], 16)

            def load_x(b, parity):
                for t in range(TILES):
                    sp.dma_start(x1[:, parity, t, :], x[b, t]).then_inc(x_loaded[t], 16)

            load_heads(0, 0)
            load_heads(0, 1)
            with nc.allow_non_contiguous_dma(reason="512 mixing factors onto partitions, once"):
                sp.dma_start(mu["k"][:, :], mu_k.rearrange("(c p) -> p c", p=P)).then_inc(small_loaded, 16)
                sp.dma_start(mu["r"][:, :], mu_r.rearrange("(c p) -> p c", p=P)).then_inc(small_loaded, 16)
            for i, g in enumerate((g_attn, g_mix)):
                sp.dma_start(tanh_g[:, i:i + 1], g.rearrange("(a n) -> a n", a=1).to_broadcast([P, 1])).then_inc(small_loaded, 16)
            for c, (n, i) in enumerate(chunks[4:], start=4):
                m = c - 4
                if chunks[m][0] == "o":
                    sp.wait_ge(w_lo, m + 1)
                else:
                    sp.wait_ge(w_turned, m + 1 - ET)
                src = wo[i] if n == "o" else {"k": w_k, "r": w_r, "v": w_v}[n][i]
                sp.dma_start(staged[:, c % 4, :], src).then_inc(w_loaded[c % 4], 16)
                if c in (ET - 1, ET + 1):
                    load_heads(0, 2 + (c - ET + 1) // 2)
                if c == ET + 1:
                    load_x(0, 0)
            for t in range(TILES):
                load_heads(1, t)
            for n in stored:
                sp.sem_inc(n, 16 * TILES)

            def batch(two, parity, has_next, has_second):
                b = 2 * two + parity
                if has_next:
                    sp.wait_ge(stored[1 - parity], 16 * TILES * two + 16 * TILES * (parity + 1))
                    load_x(b + 1, 1 - parity)
                if has_second:
                    for t in range(TILES):
                        load_heads(b + 2, t)
                for t in range(TILES):
                    sp.wait_ge(finished, TILES * b + (t + 1))
                    sp.dma_start(out[b, t], x1[:, parity, t, :]).then_inc(stored[parity], 16)

            all_batches(sp, batch)
            for s in stored:
                sp.wait_ge(s, 16 * TILES * (batches // 2 + 1))

        @block.tensor
        def _(pe):
            def products(bank, left, right, count):
                n = 0
                for i in range(count):
                    for a, c in PRODUCTS:
                        last = pe.matmul(bank[:, :], left(a, i), right(c, i), start=n == 0, stop=n == 3 * count - 1)
                        n += 1
                return last

            def project(b, t):
                pe.wait_ge(heads_lo, TILES * b + (t + 1))
                if not (isinstance(b, int) and TILES * b + t < 2):
                    pe.wait_ge(x1_ready, TILES * b + (t - 1))
                products(proj_ps[t % 2], lambda a, i: heads_p[:, t % 2, a, i, :], lambda c, i: wo_p[:, c, i, :],
                         ET).then_inc(proj_full, 1)

            def turn(b, t):
                pe.wait_ge(xn_ready, TILES * b + (t + 1))
                if not (isinstance(b, int) and TILES * b + t < 2):
                    pe.wait_ge(tr_done, TILES * b + (t - 1))
                for d in range(DT):
                    last = pe.transpose(tr_ps[t % 2][:, d * P:(d + 1) * P], xn[:, t, d * P:(d + 1) * P], ident[:, :])
                last.then_inc(tr_full, 1)

            def k_product(b, c):
                if c == 0:
                    pe.wait_ge(mix_lo, 2 * TILES * b + TILES)
                pe.wait_ge(gated, TILES * b + (c + 1))
                products(mix_ps[c], lambda a, i: wT["k"][:, a, i, c * P:(c + 1) * P], lambda e, i: mixT["k"][:, e, i, :],
                         DT).then_inc(k_full, 1)

            def r_product(b, t):
                if t == 0:
                    pe.wait_ge(mix_lo, 2 * TILES * b + 2 * TILES)
                pe.wait_ge(relu_done, TILES * b + (t + 1))
                products(mix_ps[t], lambda a, i: mixT["r"][:, a, i, t * P:(t + 1) * P], lambda e, i: wT["r"][:, e, i, :],
                         DT).then_inc(r_full, 1)

            def v_product(b, t):
                if t == 0:
                    pe.wait_ge(act_lo, TILES * b + (TILES + 2))
                pe.wait_ge(gate_done, TILES * b + (t + 1))
                products(mix_ps[t], lambda a, i: actT[:, a, i, t * P:(t + 1) * P], lambda e, i: wT["v"][:, e, i, :],
                         DT).then_inc(v_full, 1)

            def turn_chunk(c):
                pe.wait_ge(w_loaded[c % 4], 16 * (c // 4 + 1))
                if c - ET >= 2:
                    pe.wait_ge(w_lo, c - 1)
                for d in range(DT):
                    last = pe.transpose(tr_ps[c % 2][:, d * P:(d + 1) * P], staged[:, c % 4, d * P:(d + 1) * P], ident[:, :])
                last.then_inc(w_turned, 1)

            pe.wait_ge(const_done, 1)
            pe.wait_ge(heads_lo, 2)
            for e in range(ET):
                pe.wait_ge(w_lo, e + 1)
                for t in range(2):
                    for n, (a, c) in enumerate(PRODUCTS):
                        last = pe.matmul(proj_ps[t][:, :], heads_p[:, t, a, e, :], wo_p[:, c, e, :],
                                         start=e == 0 and n == 0, stop=e == ET - 1 and n == 2)
                    if e == ET - 1:
                        last.then_inc(proj_full, 1)
            for t in (2, 3):
                turn_chunk(ET + 2 * (t - 2))
                turn_chunk(ET + 2 * (t - 2) + 1)
                project(0, t)
            for c in range(ET + 4, ET + EARLY):
                turn_chunk(c)
            pe.wait_ge(w_lo, ET + EARLY)
            for t in range(TILES):
                turn(0, t)
            pe.wait_ge(tr_done, TILES)
            for c in range(ET + EARLY, len(chunks)):
                turn_chunk(c)
            pe.wait_ge(w_lo, len(chunks))

            def batch(two, parity, has_next, has_second):
                b = 2 * two + parity
                for t in range(TILES):
                    k_product(b, t)
                    if has_next:
                        project(b + 1, t)
                for t in range(TILES):
                    r_product(b, t)
                if has_next:
                    for t in range(TILES):
                        turn(b + 1, t)
                for t in range(TILES):
                    v_product(b, t)

            all_batches(pe, batch)

        @block.scalar
        def _(act):
            def heads_part(b, t):
                act.wait_ge(heads_loaded[t % 2], 16 * (TILES // 2) * b + 16 * (t // 2 + 1))
                if not (isinstance(b, int) and TILES * b + t < 2):
                    act.wait_ge(proj_full, TILES * b + (t - 1))
                act.activation(heads_p[:, t % 2, HI, :, :], heads_raw[:, t % 2, :, :], ACT.Copy).then_inc(heads_hi, 1)

            def turned(b, t):
                act.wait_ge(tr_full, TILES * b + (t + 1))
                act.activation(xnT[:, :, 1 + t * P:1 + (t + 1) * P], tr_ps[t % 2][:, :].rearrange("p (d n) -> p d n", n=P),
                               ACT.Copy).then_inc(tr_done, 1)

            def mix_part(b, m):
                n, d = MIXES[m]
                act.wait_ge(mix_ready, 2 * TILES * b + (m + 1))
                act.activation(mixT[n][:, HI, d, :], mixed[:, m % 2, :], ACT.Copy).then_inc(mix_hi, 1)

            def relu_k(b, c):
                act.wait_ge(k_full, TILES * b + (c + 1))
                act.wait_ge(act_lo, TILES * b + (c + 1))
                act.activation(relu[:, c % 2, :], mix_ps[c][:, :], ACT.Relu).then_inc(relu_done, 1)

            def act_part(b, c):
                act.wait_ge(squared, TILES * b + (c + 1))
                act.activation(actT[:, HI, c, :], relu[:, c % 2, :], ACT.Copy).then_inc(act_hi, 1)

            def gate_r(b, t):
                act.wait_ge(r_full, TILES * b + (t + 1))
                act.activation(gate[:, t, :], mix_ps[t][:, :], ACT.Sigmoid).then_inc(gate_done, 1)

            def chunk_hi(c):
                if c < ET:
                    act.wait_ge(w_loaded[c % 4], 16 * (c // 4 + 1))
                else:
                    act.wait_ge(w_turned, c - ET + 1)
                act.activation(split_chunk(c)[HI], chunk_source(c), ACT.Copy).then_inc(w_hi, 1)

            for t in range(2):
                heads_part(0, t)
            for c in range(ET):
                chunk_hi(c)
            act.wait_ge(small_loaded, 64)
            act.activation(tanh_g[:, :], tanh_g[:, :], ACT.Tanh).then_inc(tanh_done, 1)
            for t in (2, 3):
                heads_part(0, t)
                chunk_hi(ET + 2 * (t - 2))
                chunk_hi(ET + 2 * (t - 2) + 1)
            for c in range(ET + 4, ET + EARLY):
                chunk_hi(c)
            for t in range(2):
                heads_part(1, t)
            for t in range(TILES):
                turned(0, t)
            for m in range(2 * TILES):
                if m < len(chunks) - ET - EARLY:
                    chunk_hi(ET + EARLY + m)
                mix_part(0, m)

            def batch(two, parity, has_next, has_second):
                b = 2 * two + parity
                relu_k(b, 0)
                act_part(b, 0)
                relu_k(b, 1)
                if has_next:
                    heads_part(b + 1, 2)
                act_part(b, 1)
                relu_k(b, 2)
                if has_next:
                    heads_part(b + 1, 3)
                act_part(b, 2)
                relu_k(b, 3)
                act_part(b, 3)
                for t in range(TILES):
                    gate_r(b, t)
                    if has_second and t < 2:
                        heads_part(b + 2, t)
                if has_next:
                    for t in range(TILES):
                        turned(b + 1, t)
                    for m in range(2 * TILES):
                        mix_part(b + 1, m)

            all_batches(act, batch)

        @block.vector
        def _(dve):
            def residual(b, parity, t):
                dve.wait_ge(x_loaded[t], 16 * b + 16)
                dve.wait_ge(proj_full, TILES * b + (t + 1))
                dve.scalar_tensor_tensor(out=x1[:, parity, t, :], in0=proj_ps[t % 2][:, :], scalar=tanh_g[:, 0:1],
                                         in1=x1[:, parity, t, :], op0=ALU.mult, op1=ALU.add).then_inc(x1_ready, 1)

            def statistics(b, parity, t):
                n = 3 * TILES * b
                dve.wait_ge(x1_ready, TILES * b + (t + 1))
                dve.bn_stats(stats[:, t, :], x1[:, parity, t, :]).then_inc(ln_step, 1)
                wait_alone(dve, ln_step, n + (3 * t + 1), dve_passed)
                dve.bn_aggr(mean_var[:, t, :], stats[:, t, :]).then_inc(ln_step, 1)
                dve.wait_ge(ln_step, n + (3 * t + 2))
                dve.tensor_scalar(var_eps[:, t:t + 1], mean_var[:, t, 1:2], EPS, None, ALU.add).then_inc(ln_step, 1)

            def normalise(b, parity, t):
                dve.wait_ge(rstd_ready, TILES * b + (t + 1))
                dve.tensor_scalar(xn[:, t, :], x1[:, parity, t, :], mean_var[:, t, 0:1], rstd[:, t:t + 1],
                                  ALU.subtract, ALU.mult).then_inc(xn_ready, 1)

            def mix(b, m):
                n, d = MIXES[m]
                dve.wait_ge(shift_ready, 2 * TILES * b + (m + 1))
                if not (isinstance(b, int) and b == 0 and m < 2):
                    dve.wait_ge(mix_lo, 2 * TILES * b + (m - 1))
                dve.scalar_tensor_tensor(out=mixed[:, m % 2, :], in0=xnT[:, d, 1:N + 1], scalar=mu[n][:, d:d + 1],
                                         in1=shifted[:, m % 2, :], op0=ALU.mult, op1=ALU.add).then_inc(mix_ready, 1)

            def mix_part(b, m):
                n, d = MIXES[m]
                dve.wait_ge(mix_hi, 2 * TILES * b + (m + 1))
                dve.tensor_tensor(mixT[n][:, LO, d, :], mixed[:, m % 2, :], mixT[n][:, HI, d, :].bitcast(F32),
                                  ALU.subtract).then_inc(mix_lo, 1)

            def square(b, c):
                dve.wait_ge(relu_done, TILES * b + (c + 1))
                dve.tensor_tensor(relu[:, c % 2, :], relu[:, c % 2, :], relu[:, c % 2, :], ALU.mult).then_inc(squared, 1)

            def act_part(b, c):
                dve.wait_ge(act_hi, TILES * b + (c + 1))
                dve.tensor_tensor(actT[:, LO, c, :], relu[:, c % 2, :], actT[:, HI, c, :].bitcast(F32),
                                  ALU.subtract).then_inc(act_lo, 1)

            def gate_v(b, t):
                dve.wait_ge(v_full, TILES * b + (t + 1))
                dve.tensor_tensor(gate[:, t, :], mix_ps[t][:, :], gate[:, t, :], ALU.mult).then_inc(gated, 1)

            def finish(b, parity, t):
                dve.wait_ge(gated, TILES * b + (t + 1 + TILES))
                dve.scalar_tensor_tensor(out=x1[:, parity, t, :], in0=gate[:, t, :], scalar=tanh_g[:, 1:2],
                                         in1=x1[:, parity, t, :], op0=ALU.mult, op1=ALU.add).then_inc(finished, 1)

            dve.memset(xnT[:, :, 0:1], 0.0).then_inc(small_done, 1)
            dve.wait_ge(small_loaded, 64)
            for n in "kr":
                dve.tensor_scalar(one_minus_mu[n][:, :], mu[n][:, :], -1.0, 1.0, ALU.mult, ALU.add).then_inc(small_done, 1)
            dve.sem_inc(act_lo, 2)
            dve.sem_inc(gated, TILES)

            def chunk_lo(c):
                dve.wait_ge(w_hi, c + 1)
                hi, lo = split_chunk(c)
                dve.tensor_tensor(lo, chunk_source(c), hi.bitcast(F32), ALU.subtract).then_inc(w_lo, 1)

            for t in range(2):
                dve.wait_ge(heads_hi, t + 1)
                dve.tensor_tensor(heads_p[:, t, LO, :, :], heads_raw[:, t, :, :], heads_p[:, t, HI, :, :].bitcast(F32),
                                  ALU.subtract).then_inc(heads_lo, 1)
            for c in range(ET):
                chunk_lo(c)
            dve.wait_ge(tanh_done, 1)
            for t in range(TILES):
                residual(0, 0, t)
                statistics(0, 0, t)
                for c in range(ET + t * EARLY // 4, ET + (t + 1) * EARLY // 4):
                    chunk_lo(c)
            for t in range(TILES):
                normalise(0, 0, t)
            for m in range(2 * TILES):
                mix(0, m)
                if m >= 1:
                    mix_part(0, m - 1)
                if m < len(chunks) - ET - EARLY:
                    chunk_lo(ET + EARLY + m)
            mix_part(0, 2 * TILES - 1)

            def batch(two, parity, has_next, has_second):
                b = 2 * two + parity
                for t in range(TILES):
                    square(b, t)
                    if has_next and t >= 1:
                        normalise(b + 1, 1 - parity, t - 1)
                    act_part(b, t)
                    if has_next:
                        residual(b + 1, 1 - parity, t)
                        statistics(b + 1, 1 - parity, t)
                if has_next:
                    normalise(b + 1, 1 - parity, TILES - 1)
                    for m in range(TILES):
                        mix(b + 1, m)
                        if m >= 1:
                            mix_part(b + 1, m - 1)
                for t in range(TILES):
                    if has_next:
                        mix(b + 1, TILES + t)
                        mix_part(b + 1, TILES + t - 1)
                    gate_v(b, t)
                    finish(b, parity, t)
                if has_next:
                    mix_part(b + 1, 2 * TILES - 1)

            all_batches(dve, batch)

        @block.gpsimd
        def _(pool):
            def heads_part(b, t):
                pool.wait_ge(heads_hi, TILES * b + (t + 1))
                pool.tensor_tensor(out=heads_p[:, t % 2, LO, :, :], in0=heads_raw[:, t % 2, :, :],
                                   in1=heads_p[:, t % 2, HI, :, :].bitcast(F32), op=ALU.subtract).then_inc(heads_lo, 1)

            def rstds(b, t):
                pool.wait_ge(ln_step, 3 * TILES * b + 3 * (t + 1))
                pool.tensor_tensor(out=rstd[:, t:t + 1], in0=var_eps[:, t:t + 1], in1=minus_half[:, :],
                                   op=ALU.pow).then_inc(rstd_ready, 1)

            def shift(b, m):
                n, d = MIXES[m]
                if m == 0:
                    wait_alone(pool, tr_done, TILES * b + TILES, pool_passed)
                if not (isinstance(b, int) and b == 0 and m < 2):
                    wait_alone(pool, mix_ready, 2 * TILES * b + (m - 1), pool_passed)
                pool.tensor_scalar(shifted[:, m % 2, :], xnT[:, d, 0:N], one_minus_mu[n][:, d:d + 1], 1.0,
                                   ALU.mult, ALU.mult).then_inc(shift_ready, 1)

            pool.memset(minus_half[:, :], -0.5).then_inc(filled, 1)
            pool.memset(ident[:, :], 0.0).then_inc(filled, 1)
            pool.wait_ge(filled, 2)
            pool.affine_select(out=ident[:, :], in_=ident[:, :], compare_op=ALU.not_equal, fill=1.0, base=0,
                               pattern=[[-1, P]], channel_multiplier=1).then_inc(const_done, 1)
            for t in (2, 3):
                heads_part(0, t)
            for t in range(TILES):
                rstds(0, t)
            pool.wait_ge(small_done, 3)
            for m in range(2 * TILES):
                shift(0, m)
                if m in (TILES, TILES + 2):
                    heads_part(1, (m - TILES) // 2)

            def batch(two, parity, has_next, has_second):
                b = 2 * two + parity
                if has_next:
                    rstds(b + 1, 0)
                    heads_part(b + 1, 2)
                    rstds(b + 1, 1)
                    heads_part(b + 1, 3)
                    rstds(b + 1, 2)
                    rstds(b + 1, 3)
                if has_second:
                    heads_part(b + 2, 0)
                    heads_part(b + 2, 1)
                if has_next:
                    for m in range(2 * TILES):
                        shift(b + 1, m)

            all_batches(pool, batch)


def build(nc, x, ctx_in, g_attn, g_mix, wq, wk, wv, wo, w_r, w_k, w_v, mu_r, mu_k, out):
    batches, S, D = x.shape
    E = wq.shape[1]
    assert S == TILES * P and E == 2 * HEAD * PAIRS
    heads = nc.dram_tensor("heads", (batches, TILES, P, PAIRS, P), F32, kind="Internal").ap()

    def tiled(a):
        return a.rearrange("b (t p) n -> b t p n", p=P)

    def rows(a):
        return a.rearrange("(t p) n -> t p n", p=P)

    with ExitStack() as es:
        staged = es.enter_context(nc.sbuf_tensor("staged", [P, TILES, D], F32))
        staged_loaded = [es.enter_context(nc.semaphore(f"staged_loaded{i}")) for i in range(TILES)]
        attention(nc, tiled(x), tiled(ctx_in), rows(wq), rows(wk), rows(wv), heads, staged, staged_loaded, rows(wo))
        channel_mix(nc, tiled(x), heads, rows(wo), rows(w_r), rows(w_k), rows(w_v), mu_r, mu_k, g_attn, g_mix, tiled(out),
                    staged, staged_loaded)


INPUTS = ["x", "ctx_1024", "g_xattn", "g_ffn", "L0_xattn_Wq", "L0_xattn_Wk", "L0_xattn_Wv", "L0_xattn_Wo",
          "L0_ffn_W_r", "L0_ffn_W_k", "L0_ffn_W_v", "L0_ffn_mu_r", "L0_ffn_mu_k"]


def kernel(**inputs):
    import numpy as np
    import concourse.bacc as bacc
    from concourse.bass_utils import run_bass_kernel_spmd

    nc = bacc.Bacc("TRN2", target_bir_lowering=False, num_devices=1)
    arrays, args = {}, []
    for name in INPUTS:
        a = np.ascontiguousarray(inputs[name])
        arrays[f"in_{name}"] = a
        args.append(nc.dram_tensor(f"in_{name}", a.shape, mybir.dt.from_np(a.dtype), kind="ExternalInput").ap())
    out = nc.dram_tensor("out_x", arrays["in_x"].shape, F32, kind="ExternalOutput").ap()
    build(nc, *args, out)
    result = run_bass_kernel_spmd(nc, [arrays], core_ids=[0])
    return result.results[0]["out_x"]
```
